# Optimizing a Trainium2 kernel written in Bass

```python
import numpy as np
import jax
import jax.numpy as jnp

def _softmax(x, axis=-1):
    return jax.nn.softmax(x, axis=axis)

def _gelu(x):
    return jax.nn.gelu(x, approximate=True)

def _silu(x):
    return jax.nn.silu(x)

def _sigmoid(x):
    return jax.nn.sigmoid(x)

def _layernorm(x, axis=-1, eps=1e-05):
    m = jnp.mean(x, axis=axis, keepdims=True)
    v = jnp.var(x, axis=axis, keepdims=True)
    return (x - m) / jnp.sqrt(v + eps)

def _scatter_add(tgt, idx, src, axis=0):
    return tgt.at[idx].add(src)

def _segment_sum(src, seg, n):
    return jax.ops.segment_sum(src, seg, n)
kernel_name = 'mk_gnn_resnorm_d2_gnn_r8_4a3621'

def setup_inputs(seed: int=0):
    np.random.seed(seed)
    _w = jnp.asarray

    def _rec_inputs():
        import jax
        import jax.numpy as jnp
        _gk = jax.random.key(seed)
        x = -0.000202 + 1 * jax.random.normal(jax.random.fold_in(_gk, 1), (12500, 64), jnp.float32)
        _s = jax.random.randint(jax.random.fold_in(_gk, 2), (200000,), 0, 12500, jnp.int32)
        _d = jax.random.randint(jax.random.fold_in(_gk, 3), (200000,), 0, 12500, jnp.int32)
        _loop = jnp.arange(12500, dtype=jnp.int32)
        src = jnp.concatenate([_s, _d, _loop])
        dst = jnp.concatenate([_d, _s, _loop])
        _o = jnp.argsort(dst, stable=True)
        src = src[_o]
        dst = dst[_o]
        return (x, src, dst)
    x, src, dst = _rec_inputs()

    def _L0_gnn_setup():
        import jax, jax.numpy as jnp
        import numpy as np
        N_NODES = 12500
        N_EDGES = 150000
        HID = 64
        N_LAYERS = 3
        GAMMA = -0.45
        ZETA = 1.05
        key = jax.random.key(seed)
        ks = jax.random.split(key, 8)
        s = 0.05
        return {'features': jax.random.normal(ks[0], (N_NODES, HID), jnp.float32), 'nb_W': jax.random.normal(ks[1], (N_LAYERS, HID, HID), jnp.float32) * s, 'nb_b': jnp.zeros((N_LAYERS, HID), jnp.float32), 'self_W': jax.random.normal(ks[2], (N_LAYERS, HID, HID), jnp.float32) * s, 'self_b': jnp.zeros((N_LAYERS, HID), jnp.float32), 'att1_W': jax.random.normal(ks[3], (N_LAYERS, 2 * HID, HID), jnp.float32) * s, 'att1_b': jnp.zeros((N_LAYERS, HID), jnp.float32), 'att2_W': jax.random.normal(ks[4], (N_LAYERS, HID, 1), jnp.float32) * s, 'att2_b': jnp.zeros((N_LAYERS, 1), jnp.float32), 'row': jax.random.randint(ks[5], (N_EDGES,), 0, N_NODES, jnp.int32), 'col': jax.random.randint(ks[6], (N_EDGES,), 0, N_NODES, jnp.int32)}
    _L0_gnn_all = _L0_gnn_setup()
    _L0_gnn_in = {k: v for k, v in _L0_gnn_all.items() if k in ('nb_W', 'nb_b', 'self_W', 'self_b', 'att1_W', 'att1_b', 'att2_W', 'att2_b')}
    del _L0_gnn_all

    def _L1_gnn_setup():
        import jax, jax.numpy as jnp
        import numpy as np
        N_NODES = 12500
        N_EDGES = 156250
        D_FEAT = 64
        UNITS = 64
        key = jax.random.key(seed)
        k1, k2, k3 = jax.random.split(key, 3)
        features = jax.random.normal(k1, (N_NODES, D_FEAT), dtype=jnp.float32)
        edge_index = jax.random.randint(k2, (2, N_EDGES), 0, N_NODES, dtype=jnp.int64)
        weight = jax.random.normal(k3, (D_FEAT, UNITS), dtype=jnp.float32) * (1.0 / np.sqrt(D_FEAT))
        bias = jnp.zeros((UNITS,), dtype=jnp.float32)
        return {'features': features, 'edge_index': edge_index, 'weight': weight, 'bias': bias}
    _L1_gnn_all = _L1_gnn_setup()
    _L1_gnn_in = {k: v for k, v in _L1_gnn_all.items() if k in ('weight', 'bias')}
    del _L1_gnn_all
    return {'x': x, 'src': src, 'dst': dst, 'L0_gnn_nb_W': _L0_gnn_in['nb_W'], 'L0_gnn_nb_b': _L0_gnn_in['nb_b'], 'L0_gnn_self_W': _L0_gnn_in['self_W'], 'L0_gnn_self_b': _L0_gnn_in['self_b'], 'L0_gnn_att1_W': _L0_gnn_in['att1_W'], 'L0_gnn_att1_b': _L0_gnn_in['att1_b'], 'L0_gnn_att2_W': _L0_gnn_in['att2_W'], 'L0_gnn_att2_b': _L0_gnn_in['att2_b'], 'L1_gnn_weight': _L1_gnn_in['weight'], 'L1_gnn_bias': _L1_gnn_in['bias']}

def reference(x, src, dst, L0_gnn_nb_W, L0_gnn_nb_b, L0_gnn_self_W, L0_gnn_self_b, L0_gnn_att1_W, L0_gnn_att1_b, L0_gnn_att2_W, L0_gnn_att2_b, L1_gnn_weight, L1_gnn_bias):
    import jax
    import jax.numpy as jnp

    def _L0_gnn_ref(features, nb_W, nb_b, self_W, self_b, att1_W, att1_b, att2_W, att2_b, row, col):
        import jax, jax.numpy as jnp
        import numpy as np
        N_NODES = 12500
        N_EDGES = 150000
        HID = 64
        N_LAYERS = 3
        GAMMA = -0.45
        ZETA = 1.05
        n = features.shape[0]
        x = features
        out = features
        for l in range(N_LAYERS):
            f1 = jax.nn.relu(x[row] @ nb_W[l] + nb_b[l])
            f2 = jax.nn.relu(x[col] @ self_W[l] + self_b[l])
            h = jax.nn.relu(jnp.concatenate([f1, f2], axis=1) @ att1_W[l] + att1_b[l])
            log_alpha = (h @ att2_W[l] + att2_b[l])[:, 0]
            mask = jnp.clip(jax.nn.sigmoid(log_alpha) * (ZETA - GAMMA) + GAMMA, 0.0, 1.0)
            rowsum = jax.ops.segment_sum(mask, row, num_segments=n) + 1e-06
            d_inv_sqrt = jnp.clip(rowsum ** (-0.5), 0.0, 10.0)
            vals = mask * d_inv_sqrt[row] * d_inv_sqrt[col]
            x = jax.ops.segment_sum(vals[:, None] * x[col], row, num_segments=n)
            out = out + x
        return out

    def _L1_gnn_ref(features, edge_index, weight, bias):
        import jax, jax.numpy as jnp
        import numpy as np
        N_NODES = 12500
        N_EDGES = 156250
        D_FEAT = 64
        UNITS = 64
        num_nodes = features.shape[0]
        row = edge_index[0]
        col = edge_index[1]
        ones = jnp.ones(row.shape[0], dtype=features.dtype)
        degrees = jax.ops.segment_sum(ones, row, num_segments=num_nodes)
        deg_inv_sqrt = jnp.power(degrees, -0.5)
        deg_inv_sqrt = jnp.where(jnp.isfinite(deg_inv_sqrt), deg_inv_sqrt, 0.0)
        w = deg_inv_sqrt[row] * deg_inv_sqrt[col]
        msgs = features[col] * w[:, None]
        propagated = jax.ops.segment_sum(msgs, row, num_segments=num_nodes)
        h = propagated @ weight + bias
        return jax.nn.relu(h)
    edge_index = jnp.stack([src, dst])
    x = _layernorm(x + _L0_gnn_ref(x, L0_gnn_nb_W, L0_gnn_nb_b, L0_gnn_self_W, L0_gnn_self_b, L0_gnn_att1_W, L0_gnn_att1_b, L0_gnn_att2_W, L0_gnn_att2_b, src, dst), axis=-1)
    x = _layernorm(x + _L1_gnn_ref(x, edge_index, L1_gnn_weight, L1_gnn_bias), axis=-1)
    return x

_drawn_inputs = setup_inputs


def setup_inputs(seed=0):
    import zlib

    import numpy as np

    out = dict(_drawn_inputs(seed))
    spreads = {'L0_gnn_nb_b': (0.0, 0.8),
     'L0_gnn_self_b': (0.0, 0.8),
     'L0_gnn_att1_b': (0.0, 0.8),
     'L0_gnn_att2_b': (0.0, 0.8),
     'L1_gnn_bias': (0.0, 0.1)}
    factors = {'L0_gnn_nb_W': 8.0, 'L0_gnn_self_W': 8.0, 'L0_gnn_att1_W': 8.0, 'L0_gnn_att2_W': 8.0}
    for name, (base, spread) in spreads.items():
        noise = np.random.default_rng([zlib.crc32(name.encode()), seed]).standard_normal(out[name].shape)
        drawn = base * np.exp(spread * noise) if base else spread * noise
        out[name] = jnp.asarray(drawn.astype(out[name].dtype))
    for name, factor in factors.items():
        out[name] = (out[name] * factor).astype(out[name].dtype)
    return out
```

```python
from contextlib import ExitStack

import concourse.bass as bass
from concourse import mybir

F32 = mybir.dt.float32
BF16 = mybir.dt.bfloat16
I32 = mybir.dt.int32
ALU = mybir.AluOpType
ACT = mybir.ActivationFunctionType
AX_X = mybir.AxisListType.X

P = 128
C = 64
GT = 4
GE = GT * P
BG = 4
BT = BG * GT
ST_ = 16
PAD = 255
GAMMA, ZETA = -0.45, 1.05
EPS = 1e-5


class Steps:

    def __init__(self, sem, base=0):
        self.sem, self.base, self.n = sem, base, 0

    def done(self, ins):
        ins.then_inc(self.sem, 1)
        self.n += 1

    def wait(self, eng):
        eng.wait_ge(self.sem, self.base + self.n)


def wait_alone(eng, sem, value):
    eng.wait_ge(sem, value)
    eng.nop(nofuse=True)


def gnn_kernel(nc, x, src, dst, nb_W, nb_b, self_W, self_b, att1_W, att1_b, att2_W, att2_b,
               l1_W, l1_b, out):
    N = x.shape[0]
    E = src.shape[0]
    L = nb_W.shape[0]
    NB = -(-N // P)
    NP = NB * P
    T = -(-(-(-E // P)) // ST_) * ST_
    EP = P * T
    NG_MAX = (EP + NB * (GE - 1)) // GE
    NI_MAX = -(-NG_MAX // BG)
    NT = NI_MAX * BT
    GJ = -(-NI_MAX * BG // P)
    NS = 8
    assert NB % 2 == 0 and NP > N and P * NT + BT < 1 << 24 and NP * 256 < 1 << 24
    assert NT <= NB * C and T <= NB * C and 4 * NB <= 512

    FULL = N // P
    REST = N - FULL * P
    LANES = E // T
    TAIL = E - LANES * T
    LA = LANES // 16 * 16

    with ExitStack() as ctx:
        def sb(name, shape, dt=F32):
            return ctx.enter_context(nc.sbuf_tensor(name, shape, dt))

        def sem(name):
            return ctx.enter_context(nc.semaphore(name))

        x_cur = sb("x_cur", [P, NB * C])
        p_node = sb("p_node", [P, NB * C])
        stage = sb("stage", [P, NB * C])
        acc = sb("acc", [P, NB * C])
        total = sb("total", [P, NB * C])
        rs = sb("rs", [P, NB, 2])
        dinv = sb("dinv", [P, NB])
        nodeA = sb("nodeA", [P, NB])
        nodeB = sb("nodeB", [P, NB])

        rowloc = sb("rowloc", [P, NT])
        mask_all = sb("mask_all", [P, NT])

        iota_n = sb("iota_n", [P, P])
        ident = sb("ident", [P, P])
        sel = sb("sel", [P, 2, GT * P])
        selT = sb("selT", [P, 2, GT * P])
        rows = sb("rows", [P, BG, GT * C])
        hid = sb("hid", [P, 2, GT * C])
        hid2 = sb("hid2", [P, 2, GT * C])
        logit = sb("logit", [P, 2, GT])
        sig = sb("sig", [P, 2, GT])
        sig2 = sb("sig2", [P, 2, GT])
        mk = sb("mk", [P, 2, GT, 2])
        ix = sb("ix", [P, BT], I32)
        gblk = sb("gblk", [1, P * GJ], I32)
        ctl = sb("ctl", [1, 4], I32)

        xs = sb("xs", [P, 2, C])
        xT = sb("xT", [C, 2, P])
        feat = sb("feat", [P, 2, P])
        wcat = sb("wcat", [C, P])
        bd = sb("bd", [P, P])
        bcat = sb("bcat", [P, 1])
        a1b = sb("a1b", [P, C])
        a2w = sb("a2w", [P, C])
        a2b = sb("a2b", [P, 1])
        wcat_all = sb("wcat_all", [C, L, P])
        bd_all = sb("bd_all", [P, L, P])
        bcat_all = sb("bcat_all", [P, L])
        a1b_all = sb("a1b_all", [P, L, C])
        a2w_all = sb("a2w_all", [P, L, C])
        a2b_all = sb("a2b_all", [P, L])
        w1 = sb("w1", [C, C])
        b1 = sb("b1", [P, C])
        eps_t = sb("eps_t", [P, 1])

        iota_b = sb("iota_b", [P, NB], BF16)
        gval = sb("gval", [P, GJ])
        gtab = sb("gtab", [P, GJ])
        gtab_i = sb("gtab_i", [P, GJ], I32)
        onehot = sb("onehot", [P, 4, 4 * NB], BF16)
        ones_bf = sb("ones_bf", [P, P], BF16)
        before = sb("before", [P, P], BF16)
        notbefore = sb("notbefore", [P, P], BF16)
        digits_w = sb("digits_w", [1, 3, P], BF16)
        prod = sb("prod", [P, 4 * NB])
        posf = sb("posf", [P, 2, 8])
        adr_w = sb("adr_w", [P, 4, 8], I32)
        adr = sb("adr", [P, 2, 8], I32)
        val = sb("val", [P, 2, 8], I32)
        src_i = p_node[:, 0:T].bitcast(I32)
        dst_i = stage[:, 0:T].bitcast(I32)
        blk_i = total[:, 0:T].bitcast(I32)
        val_i = acc[:, 0:T].bitcast(I32)
        fill_i = mask_all[:, 0:NT].bitcast(I32)
        packed = p_node[:, 0:NT].bitcast(I32)
        col_i = acc[:, 0:NT].bitcast(I32)
        low_i = stage[:, 0:NT].bitcast(I32)
        o = [0]

        def take(k, dt=F32):
            o[0] += k
            return rowloc[:, o[0] - k:o[0]].bitcast(dt)

        cnt = take(NS * NB)
        base = take(NS * NB)
        base_i = take(NS * NB, I32)
        digit_i = take(NS * NB, I32)
        tot = take(NB)
        grp_i = take(NB, I32)
        grp = take(NB)
        gcum = take(NB)
        digits = [sb(f"digits{d}", [1, NS * NB], BF16) for d in range(3)]
        cmp_g = onehot[:, 0:2, :].rearrange("p a b -> p (a b)")[:, 0:GJ * (NB - 1)]
        assert o[0] <= NT and GJ * (NB - 1) <= 8 * NB

        banks = [ctx.enter_context(nc.psum_tensor(f"bank{i}", [P, 512], F32)) for i in range(8)]

        sorted_d = nc.dram_tensor("sorted_edges", [P * NT, 1], I32, kind="Internal").ap()
        col_d = nc.dram_tensor("sorted_cols", [P, NT], I32, kind="Internal").ap()
        gtab_d = nc.dram_tensor("group_blocks", [P, GJ], I32, kind="Internal").ap()
        q_d = nc.dram_tensor("q_table", [NP, C], F32, kind="Internal").ap()
        xd_d = nc.dram_tensor("xd_table", [NP, C], F32, kind="Internal").ap()

        const_ready = sem("const_ready")
        ones_ready = sem("ones_ready")
        pad_set = sem("pad_set")
        x_in = sem("x_in")
        edges_in = sem("edges_in")
        weights_in = sem("weights_in")
        fill_out = sem("fill_out")
        sv = sem("sort_vector_steps")
        oh_ready = sem("onehot_ready")
        oh_used = sem("onehot_used")
        oh2_ready = sem("onehot2_ready")
        oh2_used = sem("onehot2_used")
        rank_ready = sem("rank_ready")
        rank_read = sem("rank_read")
        base_ready = sem("base_ready")
        count_zero = sem("count_zero")
        adr_ready = [sem(f"adr_ready{h}") for h in range(2)]
        scattered = [sem(f"scattered{h}") for h in range(2)]
        adr_steps = sem("adr_steps")
        gtab_ready = sem("gtab_ready")
        gtab_out = sem("gtab_out")
        ctl_ready = sem("ctl_ready")
        gblk_in = sem("gblk_in")
        packed_in = sem("packed_in")
        col_ready = sem("col_ready")
        col_out = sem("col_out")

        xs_ready = sem("xs_ready")
        xT_ps = sem("xT_in_psum")
        xT_ready = sem("xT_ready")
        f_ps = sem("feat_in_psum")
        f_ready = sem("feat_ready")
        pq_ps = sem("pq_in_psum")
        pq_read = sem("pq_read")
        layer_w = sem("layer_weights")
        q_ready = sem("q_ready")
        q_out = sem("q_out")
        xd_ready = sem("xd_ready")
        xd_out = sem("xd_out")
        nv = sem("node_vector_steps")
        root_in = sem("root_in")
        root_done = sem("root_done")

        ix1_in = [sem(f"ix1_in{h}") for h in range(2)]
        rows1_in = [sem(f"rows1_in{k}") for k in range(BG)]
        sel_ready = sem("sel_ready")
        selT_ps = sem("selT_in_psum")
        selT_ready = sem("selT_ready")
        pg_ps = sem("p_rows_in_psum")
        rows1_used = sem("rows1_used")
        hid_done = sem("hid_done")
        logit_ready = sem("logit_ready")
        sig_ready = sem("sig_ready")
        sig2_done = sem("sig2_done")
        mk_ready = sem("mk_ready")
        mask_kept = sem("mask_kept")
        rs_ps = sem("rowsum_in_psum")
        rs_added = sem("rowsum_added")

        ix2_in = [sem(f"ix2_in{h}") for h in range(2)]
        rows2_in = [sem(f"rows2_in{k}") for k in range(BG)]
        sel2_ready = sem("sel2_ready")
        seg_ps = sem("segment_in_psum")
        seg_added = sem("segment_added")
        out_ready = sem("out_ready")
        out_done = sem("out_done")

        block = ctx.enter_context(nc.Block())
        view = "p (b c) -> p b c"
        x3, p3, s3, a3, t3 = (a[:].rearrange(view, c=C) for a in (x_cur, p_node, stage, acc, total))

        def table(d):
            return d.rearrange("(b p) c -> p b c", p=P)

        @block.sync
        def _(sp):
            def edge_load(to, given):
                sp.dma_start(to[0:LA, :], given[0:LA * T].rearrange("(p t) -> p t", t=T)).then_inc(edges_in, 16)
                sp.dma_start(to[LA:LANES, :], given[LA * T:LANES * T].rearrange("(p t) -> p t", t=T)).then_inc(edges_in, 16)
                sp.dma_start(to[LANES:LANES + 1, 0:TAIL], given[LANES * T:E].rearrange("(p t) -> p t", p=1)).then_inc(edges_in, 16)

            sp.wait_ge(pad_set, 1)
            edge_load(src_i, src)
            edge_load(dst_i, dst)
            sp.wait_ge(pad_set, 2)
            sp.dma_start(sorted_d.rearrange("(p t) o -> p (t o)", t=NT), fill_i).then_inc(fill_out, 16)
            sp.dma_start(x3[:, 0:FULL, :], table(x[0:FULL * P, :])).then_inc(x_in, 16)
            sp.dma_start(x3[0:REST, FULL, :], x[FULL * P:N, :]).then_inc(x_in, 16)
            loads = [
                (wcat_all[:, :, 0:C], nb_W.rearrange("l i o -> i l o")),
                (wcat_all[:, :, C:P], self_W.rearrange("l i o -> i l o")),
                (bd_all[0:C, :, 0:C], att1_W[:, 0:C, :].rearrange("l i o -> i l o")),
                (bd_all[C:P, :, C:P], att1_W[:, C:P, :].rearrange("l i o -> i l o")),
                (a1b_all[:].rearrange("p l c -> p (l c)"), att1_b.rearrange("l c -> (l c)").partition_broadcast(P)),
                (a2w_all[:].rearrange("p l c -> p (l c)"), att2_W.rearrange("l c o -> (l c o)").partition_broadcast(P)),
                (a2b_all[:], att2_b.rearrange("l o -> (l o)").partition_broadcast(P)),
                (w1[:], l1_W),
                (b1[:], l1_b.partition_broadcast(P)),
            ]
            for to, given in loads:
                sp.dma_start(to, given).then_inc(weights_in, 16)
            for l in range(L):
                sp.dma_start(bcat_all[0:C, l:l + 1], nb_b[l].rearrange("(c o) -> c o", o=1)).then_inc(weights_in, 16)
                sp.dma_start(bcat_all[C:P, l:l + 1], self_b[l].rearrange("(c o) -> c o", o=1)).then_inc(weights_in, 16)

            sp.wait_ge(gtab_ready, 1)
            sp.dma_start(gtab_d, gtab_i[:]).then_inc(gtab_out, 16)
            sp.wait_ge(gtab_out, 16)
            sp.dma_start(gblk[:], gtab_d.rearrange("(o p) j -> o (p j)", o=1)).then_inc(gblk_in, 16)
            for h in range(2):
                sp.wait_ge(scattered[h], (T // ST_) * 8 * 16)
            sp.dma_start(packed, sorted_d.rearrange("(p t) o -> p (t o)", t=NT)).then_inc(packed_in, 16)
            sp.wait_ge(col_ready, 1)
            sp.dma_start(col_d, col_i).then_inc(col_out, 16)
            sp.wait_ge(col_out, 16)

            sp.wait_ge(ctl_ready, 1)
            n_it = sp.value_load(ctl[0:1, 0:1], min_val=1, max_val=NI_MAX)

            def index_loads(first, ix_in, rows_in):
                with sp.Fori(0, n_it) as i:
                    it = sp.snap(first + i)
                    for h in range(2):
                        sp.wait_ge(rows_in[2 * h], it * 64)
                        sp.wait_ge(rows_in[2 * h + 1], it * 64)
                        sp.dma_start(ix[:, 8 * h:8 * h + 8], col_d[:, bass.ds(i * BT + 8 * h, 8)]).then_inc(ix_in[h], 16)

            with sp.Fori(0, L) as l:
                for k in range(BG):
                    wait_alone(sp, rows2_in[k], l * n_it * 64)
                sp.wait_ge(q_ready, l + 1)
                sp.dma_start(table(q_d), s3).then_inc(q_out, 16)
                index_loads(l * n_it, ix1_in, rows1_in)
                for k in range(BG):
                    sp.wait_ge(rows1_in[k], (l + 1) * n_it * 64)
                sp.wait_ge(xd_ready, l + 1)
                sp.dma_start(table(xd_d), s3).then_inc(xd_out, 16)
                index_loads(l * n_it, ix2_in, rows2_in)
            sp.wait_ge(xd_ready, L + 1)
            sp.dma_start(table(xd_d), s3).then_inc(xd_out, 16)
            index_loads(L * n_it, ix2_in, rows2_in)

            sp.wait_ge(out_ready, 1)
            sp.dma_start(table(out[0:FULL * P, :]), a3[:, 0:FULL, :]).then_inc(out_done, 16)
            sp.dma_start(out[FULL * P:N, :], a3[0:REST, FULL, :]).then_inc(out_done, 16)
            sp.wait_ge(out_done, 32)

        @block.gpsimd
        def _(pool):
            nc.gpsimd.memset(ones_bf[:], 1.0)
            nc.gpsimd.memset(ident[:], 1.0)
            for d in range(3):
                nc.gpsimd.memset(digits_w[:, d, :], float(256 ** d))
            nc.gpsimd.memset(eps_t[:], EPS)
            nc.gpsimd.memset(mk[:], 1.0).then_inc(ones_ready, 1)
            nc.gpsimd.iota(iota_b[:], [[1, NB]], base=0, channel_multiplier=0, allow_small_or_imprecise_dtypes=True)
            nc.gpsimd.iota(iota_n[:], [[1, P]], base=0, channel_multiplier=0, allow_small_or_imprecise_dtypes=True)
            nc.gpsimd.iota(gval[:], [[1, GJ]], base=0, channel_multiplier=GJ, allow_small_or_imprecise_dtypes=True)
            pool.wait_ge(ones_ready, 1)
            nc.gpsimd.affine_select(out=before[:], in_=ones_bf[:], pattern=[[1, P]], compare_op=ALU.is_gt,
                                    fill=0.0, base=0, channel_multiplier=-1)
            nc.gpsimd.affine_select(out=notbefore[:], in_=ones_bf[:], pattern=[[-1, P]], compare_op=ALU.is_ge,
                                    fill=0.0, base=0, channel_multiplier=1)
            nc.gpsimd.affine_select(out=ident[:], in_=ident[:], pattern=[[-1, P]], compare_op=ALU.is_equal,
                                    fill=0.0, base=0, channel_multiplier=1).then_inc(const_ready, 1)

            pool.wait_ge(fill_out, 16)
            with pool.Fori(0, T // ST_) as i:
                for h in range(2):
                    wait_alone(pool, adr_ready[h], i + 1)
                    for j in range(8):
                        nc.gpsimd.indirect_dma_start(
                            out=sorted_d, out_offset=bass.IndirectOffsetOnAxis(ap=adr[:, h, j:j + 1], axis=0),
                            in_=val[:, h, j:j + 1], in_offset=None).then_inc(scattered[h], 16)

            pool.wait_ge(ctl_ready, 1)
            n_it = pool.value_load(ctl[0:1, 0:1], min_val=1, max_val=NI_MAX)

            def gathers(first, table_d, ix_in, rows_in, used):
                with pool.Fori(0, n_it) as i:
                    it = pool.snap(first + i)
                    for k in range(BG):
                        if k % 2 == 0:
                            pool.wait_ge(ix_in[k // 2], (it + 1) * 16)
                        wait_alone(pool, used, it * BG + k + 1)
                        for j in range(GT):
                            t = GT * k + j
                            nc.gpsimd.indirect_dma_start(
                                out=rows[:, k, j * C:(j + 1) * C], out_offset=None, in_=table_d,
                                in_offset=bass.IndirectOffsetOnAxis(ap=ix[:, t:t + 1], axis=0)).then_inc(rows_in[k], 16)

            with pool.Fori(0, L) as l:
                wait_alone(pool, q_out, (l + 1) * 16)
                gathers(l * n_it, q_d, ix1_in, rows1_in, rows1_used)
                wait_alone(pool, xd_out, (l + 1) * 16)
                gathers(l * n_it, xd_d, ix2_in, rows2_in, seg_ps)
            pool.wait_ge(xd_out, (L + 1) * 16)
            gathers(L * n_it, xd_d, ix2_in, rows2_in, seg_ps)

        @block.scalar
        def _(act):
            act.wait_ge(ctl_ready, 1)
            n_it = act.value_load(ctl[0:1, 0:1], min_val=1, max_val=NI_MAX)
            act.sem_inc(mask_kept, 2)
            act.sem_inc(selT_ready, 2)
            act.sem_inc(xT_ready, 2)
            act.sem_inc(f_ready, 2)

            def x_transposed(B, s):
                act.wait_ge(xT_ps, B + 3)
                act.wait_ge(f_ps, B + 1)
                nc.scalar.copy(xT[:, s, :], banks[s][0:C, 0:P]).then_inc(xT_ready, 1)

            def root(r):
                act.wait_ge(root_in, r)
                nc.scalar.activation(nodeB[:], nodeA[:], ACT.Sqrt).then_inc(root_done, 1)

            with act.Fori(0, L) as l:
                act.wait_ge(layer_w, l + 1)
                with act.Fori(0, NB // 2) as j:
                    B0 = act.snap(l * NB + j * 2)
                    for s in range(2):
                        x_transposed(B0 + s, s)
                    for s in range(2):
                        act.wait_ge(f_ps, B0 + s + 3)
                        act.wait_ge(pq_ps, B0 + s + 1)
                        nc.scalar.activation(feat[:, s, :], banks[2 + s][:, 0:P], ACT.Relu,
                                             bias=bcat[:, 0:1]).then_inc(f_ready, 1)
                with act.Fori(0, n_it) as i:
                    G0 = act.snap((l * n_it + i) * BG)

                    def selT_copy(k):
                        act.wait_ge(selT_ps, G0 + k + 1)
                        act.wait_ge(pg_ps, G0 + k + 1)
                        nc.scalar.copy(selT[:, k % 2, :], banks[k % 2][:, :]).then_inc(selT_ready, 1)

                    selT_copy(0)
                    for k in range(BG):
                        if k + 1 < BG:
                            selT_copy(k + 1)
                        act.wait_ge(logit_ready, G0 + k + 1)
                        nc.scalar.activation(sig[:, k % 2, :], logit[:, k % 2, :], ACT.Sigmoid,
                                             bias=a2b[:, 0:1]).then_inc(sig_ready, 1)
                        act.wait_ge(mk_ready, G0 + k + 1)
                        nc.scalar.copy(mask_all[:, bass.ds(i * BT + k * GT, GT)],
                                       mk[:, k % 2, :, 0]).then_inc(mask_kept, 1)
                root(l + 1)
            for r in range(3):
                root(L + 1 + r)
                if r == 1:
                    with act.Fori(0, NB // 2) as j:
                        B0 = act.snap(j * 2 + L * NB)
                        for s in range(2):
                            x_transposed(B0 + s, s)

        @block.tensor
        def _(pe):
            pe.sem_inc(oh_used, 4)
            pe.sem_inc(oh2_used, 4)
            pe.sem_inc(xT_ps, 2)
            pe.sem_inc(f_ps, 2)
            pe.sem_inc(pq_ps, 2)
            pe.sem_inc(pg_ps, 2)
            pe.sem_inc(rs_ps, 2)
            pe.sem_inc(seg_ps, 4)
            pe.wait_ge(const_ready, 1)
            pe.wait_ge(count_zero, 1)
            for c in range(2):
                pe.matmul(banks[c][:, 0:4 * NB], ones_bf[:], onehot[:, 0, :], start=True, stop=False,
                          skip_group_check=True).then_inc(oh_used, 1)
            with pe.Fori(0, T // ST_) as i:
                for c in range(4):
                    pe.wait_ge(oh_ready, i * 4 + c + 1)
                    pe.matmul(banks[c % 2][:, 0:4 * NB], ones_bf[:], onehot[:, c, :], start=False, stop=False,
                              skip_group_check=True).then_inc(oh_used, 1)
            pe.wait_ge(base_ready, 1)
            for c in range(2):
                for d in range(3):
                    pe.matmul(banks[2 + c][:, 0:4 * NB], digits_w[0:1, d, :],
                              digits[d][0:1, c * 4 * NB:(c + 1) * 4 * NB], start=(d == 0), stop=False,
                              skip_group_check=True)
            with pe.Fori(0, T // ST_) as i:
                for c in range(4):
                    bank = banks[2 + c % 2]
                    pe.wait_ge(oh2_ready, i * 4 + c + 1)
                    pe.matmul(bank[:, 0:4 * NB], before[:], onehot[:, c, :], start=False, stop=False,
                              skip_group_check=True).then_inc(rank_ready, 1)
                    pe.wait_ge(rank_read, i * 4 + c + 1)
                    pe.matmul(bank[:, 0:4 * NB], notbefore[:], onehot[:, c, :], start=False, stop=False,
                              skip_group_check=True).then_inc(oh2_used, 1)

            pe.wait_ge(ctl_ready, 1)
            pe.wait_ge(gblk_in, 16)
            n_it = pe.value_load(ctl[0:1, 0:1], min_val=1, max_val=NI_MAX)
            blk_regs = [pe.alloc_register(f"pe_blk{k}") for k in range(BG)]

            def transpose_x(B, s):
                pe.wait_ge(xs_ready, B + 1)
                wait_alone(pe, xT_ready, B + 1)
                pe.transpose(banks[s][0:C, 0:P], xs[:, s, :], ident[:]).then_inc(xT_ps, 1)

            def segment_sums(first):
                with pe.Fori(0, n_it) as i:
                    it = pe.snap(first + i)
                    for k in range(BG):
                        G = it * BG + k
                        pe.wait_ge(sel2_ready, G + 1)
                        pe.wait_ge(seg_added, G + 1)
                        pe.wait_ge(rows2_in[k], (it + 1) * 64)
                        for j in range(GT):
                            mm = pe.matmul(banks[k % 2][:, 0:C], sel[:, k % 2, j * P:(j + 1) * P],
                                           rows[:, k, j * C:(j + 1) * C], start=(j == 0), stop=(j == GT - 1))
                        mm.then_inc(seg_ps, 1)

            with pe.Fori(0, L) as l:
                wait_alone(pe, layer_w, l + 1)
                with pe.Fori(0, NB // 2) as j:
                    B0 = pe.snap(l * NB + j * 2)
                    for s in range(2):
                        transpose_x(B0 + s, s)
                    for s in range(2):
                        pe.wait_ge(xT_ready, B0 + s + 3)
                        pe.wait_ge(f_ready, B0 + s + 1)
                        pe.matmul(banks[2 + s][:, 0:P], wcat[:], xT[:, s, :], start=True, stop=True).then_inc(f_ps, 1)
                    for s in range(2):
                        pe.wait_ge(f_ready, B0 + s + 3)
                        pe.wait_ge(pq_read, B0 + s + 1)
                        pe.matmul(banks[4 + s][:, 0:P], feat[:, s, :], bd[:], start=True, stop=True).then_inc(pq_ps, 1)
                with pe.Fori(0, n_it) as i:
                    G0 = pe.snap((l * n_it + i) * BG)
                    pe.load(blk_regs, gblk[0:1, bass.ds(i * BG, BG)])
                    blks = [pe.snap(r, min_val=0, max_val=NB - 1) for r in blk_regs]

                    def p_rows(k):
                        pe.wait_ge(sel_ready, G0 + k + 1)
                        pe.wait_ge(selT_ready, G0 + k + 1)
                        for j in range(GT):
                            mm = pe.transpose(banks[k % 2][:, j * P:(j + 1) * P], sel[:, k % 2, j * P:(j + 1) * P], ident[:])
                        mm.then_inc(selT_ps, 1)
                        pe.wait_ge(selT_ready, G0 + k + 3)
                        pe.wait_ge(rows1_used, G0 + k + 3)
                        for j in range(GT):
                            mm = pe.matmul(banks[2 + k % 2][:, j * C:(j + 1) * C], selT[:, k % 2, j * P:(j + 1) * P],
                                           p_node[:, bass.ds(blks[k] * C, C)], start=True, stop=True)
                        mm.then_inc(pg_ps, 1)

                    p_rows(0)
                    for k in range(BG):
                        if k + 1 < BG:
                            p_rows(k + 1)
                        pe.wait_ge(mk_ready, G0 + k + 1)
                        pe.wait_ge(rs_added, G0 + k + 1)
                        for j in range(GT):
                            mm = pe.matmul(banks[4 + k % 2][:, 0:2], sel[:, k % 2, j * P:(j + 1) * P],
                                           mk[:, k % 2, j, :], start=(j == 0), stop=(j == GT - 1))
                        mm.then_inc(rs_ps, 1)
                segment_sums(l * n_it)
            segment_sums(L * n_it)
            with pe.Fori(0, NB // 2) as j:
                B0 = pe.snap(j * 2 + L * NB)
                for s in range(2):
                    transpose_x(B0 + s, s)
                for s in range(2):
                    pe.wait_ge(xT_ready, B0 + s + 3)
                    pe.wait_ge(pq_read, B0 + s + 1)
                    pe.matmul(banks[2 + s][:, 0:C], xT[:, s, :], w1[:], start=True, stop=True).then_inc(f_ps, 1)

        @block.vector
        def _(dve):
            v = nc.vector
            pad_lane = (LANES // 32) * 32
            v.memset(src_i[pad_lane:P, :], float(NP - 1))
            v.memset(dst_i[pad_lane:P, :], 0.0).then_inc(pad_set, 1)
            v.memset(fill_i, float(PAD))
            v.memset(x3[:, FULL:NB, :], 0.0)
            v.memset(bd_all[:], 0.0).then_inc(pad_set, 1)
            v.memset(onehot[:, 0, :], 0.0).then_inc(count_zero, 1)
            for s, n in ((pq_read, 2), (rows1_used, 4), (rs_added, 2), (seg_added, 2)):
                dve.sem_inc(s, n)

            st = Steps(sv)
            dve.wait_ge(edges_in, 96)
            v.tensor_scalar(blk_i, src_i, 7, None, ALU.logical_shift_right)
            st.done(v.tensor_scalar(src_i, src_i, P - 1, None, ALU.bitwise_and))
            st.wait(dve)
            st.done(v.scalar_tensor_tensor(val_i, dst_i, 256.0, src_i, ALU.mult, ALU.add))
            st.wait(dve)
            dve.wait_ge(const_ready, 1)
            dve.wait_ge(oh_used, 6)

            def one_hot(i, c):
                keys = blk_i[:, bass.ds(i * ST_ + 4 * c, 4)].unsqueeze(2).to_broadcast([P, 4, NB])
                ids = iota_b[:].unsqueeze(1).to_broadcast([P, 4, NB])
                return v.tensor_tensor(onehot[:, c, :].rearrange("p (t b) -> p t b", b=NB), keys, ids, ALU.is_equal)

            with dve.Fori(0, T // ST_) as i:
                for c in range(4):
                    dve.wait_ge(oh_used, i * 4 + c + 3)
                    one_hot(i, c).then_inc(oh_ready, 1)

            dve.wait_ge(oh_used, 6 + T // 4)
            for c in range(2):
                st.done(v.tensor_copy(cnt[:, c * 4 * NB:(c + 1) * 4 * NB], banks[c][:, 0:4 * NB]))
            st.wait(dve)
            st.done(v.tensor_reduce(tot, cnt.rearrange("p (s b) -> p b s", b=NB), AX_X, ALU.add))
            st.wait(dve)
            st.done(v.tensor_scalar(grp_i, tot, float(GE - 1), None, ALU.add))
            st.wait(dve)
            st.done(v.tensor_scalar(grp_i, grp_i, 9, None, ALU.logical_shift_right))
            st.wait(dve)
            st.done(v.tensor_copy(grp, grp_i))
            st.done(v.memset(tot, 1.0))
            st.wait(dve)
            st.done(v.tensor_tensor_scan(gcum, tot, grp, 0.0, ALU.mult, ALU.add))
            st.wait(dve)
            st.done(v.tensor_scalar(ctl[0:1, 1:2], gcum[0:1, NB - 1:NB], float(BG - 1), None, ALU.add))
            st.done(v.tensor_tensor(grp, gcum, grp, ALU.subtract))
            st.wait(dve)
            v.tensor_scalar(ctl[0:1, 0:1], ctl[0:1, 1:2], 2, None, ALU.logical_shift_right).then_inc(ctl_ready, 1)
            st.done(v.tensor_scalar(base[:, 0:NB], grp, float(GE), None, ALU.mult))
            for s in range(1, NS):
                st.wait(dve)
                st.done(v.tensor_tensor(base[:, s * NB:(s + 1) * NB], base[:, (s - 1) * NB:s * NB],
                                        cnt[:, (s - 1) * NB:s * NB], ALU.add))
            st.wait(dve)
            st.done(v.tensor_copy(base_i[0:1, :], base[0:1, :]))
            st.wait(dve)
            for d in range(3):
                st.done(v.tensor_scalar(digit_i[0:1, :], base_i[0:1, :], 8 * d, 255, ALU.logical_shift_right, ALU.bitwise_and))
                st.wait(dve)
                st.done(v.tensor_copy(digits[d][:], digit_i[0:1, :]))
                st.wait(dve)
            dve.sem_inc(base_ready, 1)
            cmp3 = cmp_g.rearrange("p (j b) -> p j b", b=NB - 1)
            st.done(v.tensor_tensor(cmp3, gval[:].unsqueeze(2).to_broadcast([P, GJ, NB - 1]),
                                    gcum[:, 0:NB - 1].unsqueeze(1).to_broadcast([P, GJ, NB - 1]), ALU.is_ge))
            st.wait(dve)
            st.done(v.tensor_reduce(gtab[:], cmp3, AX_X, ALU.add))
            st.wait(dve)
            v.tensor_copy(gtab_i[:], gtab[:]).then_inc(gtab_ready, 1)

            ADR = 2 * 5
            with dve.Fori(0, T // ST_) as i:
                ad = Steps(adr_steps, i * ADR)
                for h in range(2):
                    for c in (2 * h, 2 * h + 1):
                        dve.wait_ge(oh2_used, i * 4 + c + 1)
                        one_hot(i, c).then_inc(oh2_ready, 1)
                        dve.wait_ge(rank_ready, i * 4 + c + 1)
                        dve.wait_ge(oh2_ready, i * 4 + c + 1)
                        v.tensor_tensor(prod[:], banks[2 + c % 2][:, 0:4 * NB], onehot[:, c, :], ALU.mult).then_inc(rank_read, 1)
                        dve.wait_ge(rank_read, i * 4 + c + 1)
                        ad.done(v.tensor_reduce(posf[:, h, 4 * (c % 2):4 * (c % 2) + 4],
                                                prod[:].rearrange("p (t b) -> p t b", b=NB), AX_X, ALU.add))
                    ad.wait(dve)
                    pos, lane, tile, sub = (adr_w[:, w, :] for w in range(4))
                    ad.done(v.tensor_copy(pos, posf[:, h, :]))
                    ad.wait(dve)
                    v.tensor_scalar(lane, pos, 2, P - 1, ALU.logical_shift_right, ALU.bitwise_and)
                    v.tensor_scalar(tile, pos, 9, 2, ALU.logical_shift_right, ALU.logical_shift_left)
                    ad.done(v.tensor_scalar(sub, pos, GT - 1, None, ALU.bitwise_and))
                    wait_alone(dve, adr_steps, ad.base + ad.n)
                    ad.done(v.tensor_tensor(tile, tile, sub, ALU.add))
                    ad.wait(dve)
                    dve.wait_ge(scattered[h], i * 128)
                    v.scalar_tensor_tensor(adr[:, h, :], lane, float(NT), tile, ALU.mult, ALU.add)
                    v.tensor_copy(val[:, h, :], val_i[:, bass.ds(i * ST_ + 8 * h, 8)]).then_inc(adr_ready[h], 1)
                assert ad.n == ADR

            st = Steps(sv, st.n)
            dve.wait_ge(packed_in, 16)
            v.tensor_scalar(col_i, packed, 8, None, ALU.logical_shift_right).then_inc(col_ready, 1)
            st.done(v.tensor_scalar(low_i, packed, PAD, None, ALU.bitwise_and))
            st.wait(dve)
            st.done(v.tensor_copy(rowloc[:], low_i))
            dve.wait_ge(x_in, 32)
            st.done(v.tensor_scalar(total[:], x_cur[:], 2.0, None, ALU.mult))
            dve.wait_ge(weights_in, (9 + 2 * L) * 16)
            dve.wait_ge(col_out, 16)
            dve.wait_ge(gblk_in, 16)
            n_it = dve.value_load(ctl[0:1, 0:1], min_val=1, max_val=NI_MAX)
            blk_regs = [dve.alloc_register(f"dve_blk{k}") for k in range(BG)]
            st.wait(dve)

            def per_node(a):
                return a.unsqueeze(2).to_broadcast([P, NB, C])

            def segment_adds(first):
                with dve.Fori(0, n_it) as i:
                    G0 = dve.snap((first + i) * BG)
                    dve.load(blk_regs, gblk[0:1, bass.ds(i * BG, BG)])
                    blks = [dve.snap(r, min_val=0, max_val=NB - 1) for r in blk_regs]

                    def weighted_sel(k):
                        dve.wait_ge(seg_ps, G0 + k + 3)
                        for j in range(GT):
                            t = i * BT + (k * GT + j)
                            ins = v.tensor_scalar(sel[:, k % 2, j * P:(j + 1) * P], iota_n[:], rowloc[:, bass.ds(t, 1)],
                                                  mask_all[:, bass.ds(t, 1)], ALU.is_equal, ALU.mult)
                        ins.then_inc(sel2_ready, 1)

                    weighted_sel(0)
                    for k in range(BG):
                        if k + 1 < BG:
                            weighted_sel(k + 1)
                        dve.wait_ge(seg_ps, G0 + k + 5)
                        dve.wait_ge(seg_added, G0 + k + 2)
                        at = acc[:, bass.ds(blks[k] * C, C)]
                        v.tensor_tensor(at, at, banks[k % 2][:, 0:C], ALU.add).then_inc(seg_added, 1)

            NODE_STEPS = 15
            with dve.Fori(0, L) as l:
                ns = Steps(nv, l * NODE_STEPS)
                for to, given in ((wcat[:], wcat_all[:, bass.ds(l, 1), :]), (bd[:], bd_all[:, bass.ds(l, 1), :]),
                                  (bcat[:], bcat_all[:, bass.ds(l, 1)]), (a1b[:], a1b_all[:, bass.ds(l, 1), :]),
                                  (a2w[:], a2w_all[:, bass.ds(l, 1), :])):
                    if len(given.shape) == 3:
                        given = given.rearrange("p o c -> p (o c)")
                    v.tensor_copy(to, given)
                v.tensor_copy(a2b[:], a2b_all[:, bass.ds(l, 1)]).then_inc(layer_w, 1)
                v.memset(rs[:], 0.0)
                ns.done(v.memset(acc[:], 0.0))
                ns.wait(dve)
                dve.wait_ge(layer_w, l + 1)
                wait_alone(dve, xd_out, l * 16)

                with dve.Fori(0, NB // 2) as j:
                    B0 = dve.snap(l * NB + j * 2)
                    for s in range(2):
                        dve.wait_ge(xT_ps, B0 + s + 1)
                        v.tensor_copy(xs[:, s, :], x_cur[:, bass.ds((j * 2 + s) * C, C)]).then_inc(xs_ready, 1)
                    for s in range(2):
                        dve.wait_ge(pq_ps, B0 + s + 3)
                        at = bass.ds((j * 2 + s) * C, C)
                        v.tensor_tensor(p_node[:, at], banks[4 + s][:, 0:C], a1b[:], ALU.add)
                        v.tensor_copy(stage[:, at], banks[4 + s][:, C:2 * C]).then_inc(pq_read, 1)
                dve.wait_ge(pq_read, (l + 1) * NB + 2)
                dve.sem_inc(q_ready, 1)

                with dve.Fori(0, n_it) as i:
                    G0 = dve.snap((l * n_it + i) * BG)
                    dve.load(blk_regs, gblk[0:1, bass.ds(i * BG, BG)])
                    blks = [dve.snap(r, min_val=0, max_val=NB - 1) for r in blk_regs]

                    def plain_sel(k):
                        dve.wait_ge(rs_ps, G0 + k + 1)
                        v.tensor_tensor(sel[:, k % 2, :].rearrange("p (t n) -> p t n", n=P),
                                        iota_n[:].unsqueeze(1).to_broadcast([P, GT, P]),
                                        rowloc[:, bass.ds(i * BT + k * GT, GT)].unsqueeze(2).to_broadcast([P, GT, P]),
                                        ALU.is_equal).then_inc(sel_ready, 1)

                    def add_rowsum(k):
                        dve.wait_ge(rs_ps, G0 + k + 3)
                        dve.wait_ge(rs_added, G0 + k + 2)
                        at = rs[:, bass.ds(blks[k], 1), :].rearrange("p o c -> p (o c)")
                        v.tensor_tensor(at, at, banks[4 + k % 2][:, 0:2], ALU.add).then_inc(rs_added, 1)

                    plain_sel(0)
                    for k in range(BG):
                        s = k % 2
                        if k + 1 < BG:
                            plain_sel(k + 1)
                        dve.wait_ge(pg_ps, G0 + k + 3)
                        dve.wait_ge(rows1_in[k], (l * n_it + i + 1) * 64)
                        v.tensor_tensor(hid[:, s, :], banks[2 + s][:, 0:GT * C], rows[:, k, :], ALU.add).then_inc(rows1_used, 1)
                        dve.wait_ge(rows1_used, G0 + k + 5)
                        v.scalar_tensor_tensor(hid2[:, s, :].rearrange("p (t c) -> p t c", c=C),
                                               hid[:, s, :].rearrange("p (t c) -> p t c", c=C), 0.0,
                                               a2w[:].unsqueeze(1).to_broadcast([P, GT, C]),
                                               ALU.max, ALU.mult).then_inc(hid_done, 1)
                        if k > 0:
                            add_rowsum(k - 1)
                        dve.wait_ge(hid_done, G0 + k + 1)
                        v.tensor_reduce(logit[:, s, :], hid2[:, s, :].rearrange("p (t c) -> p t c", c=C), AX_X,
                                        ALU.add).then_inc(logit_ready, 1)
                        dve.wait_ge(sig_ready, G0 + k + 1)
                        v.tensor_scalar(sig2[:, s, :], sig[:, s, :], ZETA - GAMMA, GAMMA, ALU.mult, ALU.add).then_inc(sig2_done, 1)
                        dve.wait_ge(sig2_done, G0 + k + 1)
                        dve.wait_ge(mask_kept, G0 + k + 1)
                        v.tensor_scalar(mk[:, s, :, 0], sig2[:, s, :], 0.0, 1.0, ALU.max, ALU.min).then_inc(mk_ready, 1)
                    add_rowsum(BG - 1)

                dve.wait_ge(rs_added, (l + 1) * n_it * BG + 2)
                ns.done(v.tensor_scalar(nodeA[:], rs[:, :, 0], 1e-6, None, ALU.add))
                ns.wait(dve)
                dve.sem_inc(root_in, 1)
                dve.wait_ge(root_done, l + 1)
                ns.done(v.reciprocal(dinv[:], nodeB[:]))
                ns.wait(dve)
                ns.done(v.tensor_scalar(dinv[:], dinv[:], 10.0, 0.0, ALU.min, ALU.max))
                ns.wait(dve)
                dve.wait_ge(q_out, (l + 1) * 16)
                v.tensor_tensor(s3, x3, per_node(dinv[:]), ALU.mult).then_inc(xd_ready, 1)
                wait_alone(dve, mask_kept, (l + 1) * n_it * BG + 2)
                segment_adds(l * n_it)
                dve.wait_ge(seg_added, (l + 1) * n_it * BG + 2)
                ns.done(v.tensor_tensor(x3, a3, per_node(dinv[:]), ALU.mult))
                ns.wait(dve)
                ns.done(v.tensor_tensor(total[:], total[:], x_cur[:], ALU.add))
                ns.wait(dve)
                assert ns.n <= NODE_STEPS
                if ns.n < NODE_STEPS:
                    dve.sem_inc(nv, NODE_STEPS - ns.n)

            ns = Steps(nv, L * NODE_STEPS)

            def layer_norm(to3, z3, centered3, tmp3, r):
                ns.done(v.tensor_reduce(nodeA[:], z3, AX_X, ALU.add))
                ns.wait(dve)
                ns.done(v.tensor_scalar(nodeA[:], nodeA[:], 1.0 / C, None, ALU.mult))
                ns.wait(dve)
                ns.done(v.tensor_tensor(centered3, z3, per_node(nodeA[:]), ALU.subtract))
                ns.wait(dve)
                ns.done(v.tensor_tensor(tmp3, centered3, centered3, ALU.mult))
                ns.wait(dve)
                ns.done(v.tensor_reduce(nodeA[:], tmp3, AX_X, ALU.add))
                ns.wait(dve)
                ns.done(v.tensor_scalar(nodeA[:], nodeA[:], 1.0 / C, EPS, ALU.mult, ALU.add))
                ns.wait(dve)
                dve.sem_inc(root_in, 1)
                dve.wait_ge(root_done, r)
                ns.done(v.reciprocal(nodeA[:], nodeB[:]))
                ns.wait(dve)
                ns.done(v.tensor_tensor(to3, centered3, per_node(nodeA[:]), ALU.mult))
                ns.wait(dve)

            layer_norm(x3, t3, a3, p3, L + 1)
            ns.done(v.tensor_scalar(nodeA[:], rs[:, :, 1], 1.0, None, ALU.max))
            ns.done(v.memset(mask_all[:], 1.0))
            ns.done(v.memset(acc[:], 0.0))
            ns.wait(dve)
            dve.sem_inc(root_in, 1)
            dve.wait_ge(root_done, L + 2)
            ns.done(v.reciprocal(nodeA[:], nodeB[:]))
            ns.wait(dve)
            ns.done(v.scalar_tensor_tensor(dinv[:], rs[:, :, 1], 1.0, nodeA[:], ALU.min, ALU.mult))
            ns.wait(dve)
            dve.wait_ge(xd_out, L * 16)
            v.tensor_tensor(s3, x3, per_node(dinv[:]), ALU.mult).then_inc(xd_ready, 1)
            segment_adds(L * n_it)
            dve.wait_ge(seg_added, (L + 1) * n_it * BG + 2)
            ns.done(v.tensor_tensor(p3, a3, per_node(dinv[:]), ALU.mult))
            ns.wait(dve)
            dve.wait_ge(xd_out, (L + 1) * 16)
            with dve.Fori(0, NB // 2) as j:
                B0 = dve.snap(j * 2 + L * NB)
                for s in range(2):
                    dve.wait_ge(xT_ps, B0 + s + 1)
                    v.tensor_copy(xs[:, s, :], p_node[:, bass.ds((j * 2 + s) * C, C)]).then_inc(xs_ready, 1)
                for s in range(2):
                    dve.wait_ge(f_ps, B0 + s + 3)
                    v.tensor_tensor(stage[:, bass.ds((j * 2 + s) * C, C)], banks[2 + s][:, 0:C], b1[:],
                                    ALU.add).then_inc(pq_read, 1)
            dve.wait_ge(pq_read, (L + 1) * NB + 2)
            ns.done(v.scalar_tensor_tensor(total[:], stage[:], 0.0, x_cur[:], ALU.max, ALU.add))
            ns.wait(dve)
            layer_norm(a3, t3, s3, p3, L + 3)
            dve.sem_inc(out_ready, 1)


_INS = ['x', 'src', 'dst', 'L0_gnn_nb_W', 'L0_gnn_nb_b', 'L0_gnn_self_W', 'L0_gnn_self_b', 'L0_gnn_att1_W',
        'L0_gnn_att1_b', 'L0_gnn_att2_W', 'L0_gnn_att2_b', 'L1_gnn_weight', 'L1_gnn_bias']


def kernel(**inputs):
    import numpy as np
    import concourse.bacc as bacc
    from concourse.bass_utils import run_bass_kernel_spmd

    nc = bacc.Bacc("TRN2", target_bir_lowering=False, num_devices=1)
    arrays, args = {}, []
    for name in _INS:
        a = np.ascontiguousarray(inputs[name])
        arrays[f"in_{name}"] = a
        args.append(nc.dram_tensor(f"in_{name}", a.shape, mybir.dt.from_np(a.dtype), kind="ExternalInput").ap())
    out = nc.dram_tensor("out_0", inputs['x'].shape, F32, kind="ExternalOutput").ap()
    gnn_kernel(nc, *args, out)
    r = run_bass_kernel_spmd(nc, [arrays], core_ids=[0])
    return r.results[0]["out_0"]
```

```python
from contextlib import ExitStack

import concourse.bass as bass
from concourse import mybir

F32 = mybir.dt.float32
BF16 = mybir.dt.bfloat16
I32 = mybir.dt.int32
I16 = mybir.dt.int16
ALU = mybir.AluOpType
ACT = mybir.ActivationFunctionType
AX_X = mybir.AxisListType.X

P = 128
C = 64
PT = 2
PAIR = PT * P
GT = 4
BG = 4
BT = BG * GT
BP = BT // PT
NPL = 3
CB = 7
SORT = 16
PAD = 255
GAMMA, ZETA = -0.45, 1.05
EPS = 1e-5


class Steps:

    def __init__(self, sem, base=0):
        self.sem, self.base, self.n = sem, base, 0

    def done(self, ins):
        ins.then_inc(self.sem, 1)
        self.n += 1

    def wait(self, eng):
        eng.wait_ge(self.sem, self.base + self.n)


def wait_alone(eng, sem, value):
    eng.wait_ge(sem, value)
    eng.nop(nofuse=True)


def gnn_kernel(nc, x, src, dst, nb_W, nb_b, self_W, self_b, att1_W, att1_b, att2_W, att2_b,
               l1_W, l1_b, out):
    N = x.shape[0]
    E = src.shape[0]
    L = nb_W.shape[0]
    NB = -(-N // P)
    NP = NB * P
    T = -(-(-(-E // P)) // (2 * SORT)) * 2 * SORT
    EP = P * T
    NG_MAX = (EP + NB * (PAIR - 1)) // PAIR
    NI_MAX = -(-NG_MAX // (2 * BP)) * 2
    NT = NI_MAX * BT
    GJ = -(-NI_MAX * BP // P)
    NCH = NB // CB
    Q_STORES = NCH + 1
    NS = 8
    NLO = 8
    NHI = -(-NB // NLO)
    assert NB <= P and NB % (2 * CB) == 0 and NP > N and P * NT + BT < 1 << 24 and NP * 256 < 1 << 24
    assert NT <= NB * C and T <= NB * C and 4 * NB <= 512

    FULL = N // P
    REST = N - FULL * P
    LANES = E // T
    TAIL = E - LANES * T
    LA = LANES // 16 * 16

    LO_CHUNKS = -(-NT // P)
    LO_OUTS = (NT >= P) + (NT % P > 0)

    with ExitStack() as ctx:
        def sb(name, shape, dt=F32):
            return ctx.enter_context(nc.sbuf_tensor(name, shape, dt))

        def sem(name):
            return ctx.enter_context(nc.semaphore(name))

        x_cur = sb("x_cur", [P, NB * C])
        p_node = sb("p_node", [P, NB * NPL * C], BF16)
        stage = sb("stage", [P, NB * C])
        acc = sb("acc", [P, NB * C])
        total = sb("total", [P, NB * C])
        rs = sb("rs", [P, NB, NPL + 1])
        dinv = sb("dinv", [P, NB])
        nodeA = sb("nodeA", [P, NB])
        nodeB = sb("nodeB", [P, NB])

        rowloc = sb("rowloc", [P, NT])
        mask_all = sb("mask_all", [P, NT])

        iota_n = sb("iota_n", [P, P])
        iota_bf = sb("iota_bf", [P, P], BF16)
        ident = sb("ident", [P, P])
        ident_bf = sb("ident_bf", [P, P], BF16)
        iota_p = sb("iota_p", [P, 1])
        sel = sb("sel", [P, BG, GT * P], BF16)
        selT = sb("selT", [P, 2, GT * P], BF16)
        rows = sb("rows", [P, BG, GT * C])
        dcol = sb("dcol", [P, 2 * GT])
        hid_all = sb("hid_all", [P, 4, GT * C])
        hid, hid2 = hid_all[:, 0:2, :], hid_all[:, 2:4, :]
        logit = sb("logit", [P, BT])
        sig = sb("sig", [P, BT])
        stretched = sb("stretched", [P, BT])
        mrest = sb("mrest", [P, BT])
        mk = sb("mk", [P, BT, NPL + 1], BF16)
        ix = sb("ix", [P, BT], I32)
        gblk = sb("gblk", [1, BP + P * GJ], I16)
        ctl = sb("ctl", [1, 4], I32)

        xs = sb("xs", [P, 2, CB * C])
        xT = rows[0:C].rearrange("p k n -> p (k n)")[:, 0:CB * P]
        feat = hid_all[:].rearrange("p k n -> p (k n)")[:, 0:CB * P]
        pf = sb("pf", [P, 2, CB * C])
        rows_q3 = sb("rows_q3", [P, GT * P])
        rows_flat = rows[:].rearrange("p k n -> p (k n)")
        qx_rows = (rows_flat[:, 2 * GT * C:4 * GT * C], rows_q3[:])
        q_rows = [rows[:, k, :].rearrange("p (t c) -> p t c", c=C) for k in range(2)] + [
            a.rearrange("p (t c) -> p t c", c=P)[:, :, 0:C] for a in qx_rows]
        x_rows = [a.rearrange("p (t c) -> p t c", c=P)[:, :, C:P] for a in qx_rows]
        x_out_buf = xs[:, :, 0:GT * C]
        dinv_pl = pf[:, 0, 0:NPL * NB // 2 + 1].bitcast(BF16)
        lo_row = sel[:, 0:2, :]
        node_f32 = p_node[:].bitcast(F32)
        wsel = node_f32[:, 0:BG * GT * P].rearrange("p (s n) -> p s n", s=BG)
        x_slots = node_f32[:, BG * GT * P:BG * (GT * P + GT * C)].rearrange("p (s n) -> p s n", s=BG)
        assert BG * (GT * P + GT * C) <= NB * C
        hi = node_f32[:, NB * C:NB * C + NT // 2]
        lo_onehot = selT
        picked = [hid_all[:, 2 * g:2 * g + 2, :].rearrange("p a n -> p (a n)")[:, 0:GT * NB] for g in range(2)]
        wcat = sb("wcat", [C, P])
        bd = sb("bd", [P, P])
        bcat = sb("bcat", [P, 1])
        a1b = sb("a1b", [P, C])
        a2w = sb("a2w", [P, C])
        a2b = sb("a2b", [P, 1])
        wcat_all = sb("wcat_all", [C, L, P])
        bd_all = sb("bd_all", [P, L, P])
        bcat_all = sb("bcat_all", [P, L])
        a1b_all = sb("a1b_all", [P, L, C])
        a2w_all = sb("a2w_all", [P, L, C])
        a2b_all = sb("a2b_all", [P, L])
        w1 = sb("w1", [C, C])
        b1 = sb("b1", [P, C])

        gval = sb("gval", [P, GJ])
        gtab = sb("gtab", [P, GJ])
        gtab_i = sb("gtab_i", [P, GJ], I16)
        ones_bf = sb("ones_bf", [P, P], BF16)
        before = sb("before", [P, P], BF16)
        notbefore = sb("notbefore", [P, P], BF16)
        digits_w = sb("digits_w", [1, 3, P], BF16)
        posf = sb("posf", [P, 2, 8])
        adr_w = sb("adr_w", [P, 4, 8], I32)
        adr = sb("adr", [P, 2, 8], I32)
        val = sb("val", [P, 2, 8], I32)
        p_f32 = node_f32[:, 0:NB * C]
        src_i = p_f32[:, 0:T].bitcast(I32)
        dst_i = stage[:, 0:T].bitcast(I32)
        blk_i = total[:, 0:T].bitcast(I32)
        val_i = acc[:, 0:T].bitcast(I32)
        bhi_i, blo_i = dst_i, src_i
        hot = selT[:].rearrange("p a n -> p (a n)")
        hi_hot = hot[:, 0:2 * SORT * NHI].rearrange("p (a n) -> p a n", a=2)
        lo_hot = hot[:, 2 * SORT * NHI:2 * SORT * (NHI + NLO)].rearrange("p (a n) -> p a n", a=2)
        cnt_small = rows_q3[0:NHI, 0:NS * NLO]
        fill_i = mask_all[:, 0:NT].bitcast(I32)
        packed = p_f32[:, 0:NT].bitcast(I32)
        col_i = acc[:, 0:NT].bitcast(I32)
        low_i = stage[:, 0:NT].bitcast(I32)
        lo_f = total[:, 0:NT]
        loT = mask_all[:].bitcast(BF16)
        taken = [0]

        def take(k, dt=F32):
            taken[0] += k
            return rowloc[:, taken[0] - k:taken[0]].bitcast(dt)

        cnt = take(NS * NB)
        base = take(NS * NB)
        base_i = take(NS * NB, I32)
        digit_i = take(NS * NB, I32)
        grp_i = take(NB, I32)
        tot, grp, gcum = dinv[:], nodeA[:], nodeB[:]
        onehot = sel[:].rearrange("p a n -> p (a n)")[:, 0:16 * NB].rearrange("p (k n) -> p k n", k=4)
        prod = hid.rearrange("p a n -> p (a n)")[:, 0:4 * NB]
        digits = [a[0:1, s, 0:NS * NB // 2].bitcast(BF16) for a, s in ((xs, 0), (xs, 1), (pf, 0))]
        cmp_g = onehot.rearrange("p a b -> p (a b)")[:, 0:GJ * (NB - 1)]
        assert CB * P <= 4 * GT * C and NS * NB // 2 <= CB * C and taken[0] <= NT
        assert 16 * NB <= BG * GT * P and GJ * (NB - 1) <= 16 * NB

        warm = sb("warm", [P, 1])
        banks = [ctx.enter_context(nc.psum_tensor(f"bank{i}", [P, 512], F32)) for i in range(8)]

        seg_banks = [banks[b] for b in (0, 1, 4, 5)]

        sorted_d = nc.dram_tensor("sorted_edges", [P * NT, 1], I32, kind="Internal").ap()
        col_d = nc.dram_tensor("sorted_cols", [P, NT], I32, kind="Internal").ap()
        cnt_d = nc.dram_tensor("stream_counts", [NS, NHI * NLO], F32, kind="Internal").ap()
        hi_d = nc.dram_tensor("col_blocks", [P, NT // 2], F32, kind="Internal").ap()
        lo_d = nc.dram_tensor("cols_in_block", [NT * P], BF16, kind="Internal").ap()
        qx_d = nc.dram_tensor("qx_table", [NP, 2 * C], F32, kind="Internal").ap()
        xg_d = nc.dram_tensor("gathered_x", [P, NT // 2 * C], F32, kind="Internal").ap()
        gtab_d = nc.dram_tensor("pair_blocks", [P, GJ], I16, kind="Internal").ap()
        q_d = nc.dram_tensor("q_table", [NP, C], F32, kind="Internal").ap()
        xd_d = nc.dram_tensor("xd_table", [NP, C], F32, kind="Internal").ap()

        const_ready = sem("const_ready")
        ones_ready = sem("ones_ready")
        pad_set = sem("pad_set")
        x_in = sem("x_in")
        edges_in = sem("edges_in")
        weights_in = sem("weights_in")
        fill_out = sem("fill_out")
        sv = sem("sort_vector_steps")
        oh_ready = sem("onehot_ready")
        oh_used = sem("onehot_used")
        oh2_ready = sem("onehot2_ready")
        oh2_used = sem("onehot2_used")
        rank_ready = sem("rank_ready")
        rank_read = sem("rank_read")
        base_ready = sem("base_ready")
        counted = sem("counted")
        cnt_out = sem("counts_out")
        cnt_in = sem("counts_in")
        count_zero = sem("count_zero")
        adr_ready = [sem(f"adr_ready{h}") for h in range(2)]
        scattered = [sem(f"scattered{h}") for h in range(2)]
        adr_steps = sem("adr_steps")
        gtab_ready = sem("gtab_ready")
        gtab_out = sem("gtab_out")
        ctl_ready = sem("ctl_ready")
        gblk_in = sem("gblk_in")
        packed_in = sem("packed_in")
        col_ready = sem("col_ready")
        col_out = sem("col_out")
        lo_ready = sem("lo_ready")
        loT_ps = sem("loT_in_psum")
        loT_ready = sem("loT_ready")
        lo_out = sem("lo_out")
        hi_ready = sem("hi_ready")
        hi_out = sem("hi_out")
        hi_in = sem("hi_in")

        xs_ready = sem("xs_ready")
        xT_ps = sem("xT_in_psum")
        xT_ready = sem("xT_ready")
        f_ps = sem("feat_in_psum")
        f_ready = sem("feat_ready")
        pq_ps = sem("pq_in_psum")
        pq_read = sem("pq_read")
        plane_steps = sem("plane_steps")
        layer_w = sem("layer_weights")
        q_out = sem("q_out")
        xd_ready = sem("xd_ready")
        xd_out = sem("xd_out")
        nv = sem("node_vector_steps")
        root_in = sem("root_in")
        root_done = sem("root_done")

        ix1_in = [sem(f"ix1_in{h}") for h in range(2)]
        rows1_in = [sem(f"rows1_in{k}") for k in range(BG)]
        sel_ready = sem("sel_ready")
        selT_ps = sem("selT_in_psum")
        selT_ready = sem("selT_ready")
        pg_ps = sem("p_rows_in_psum")
        rows1_used = sem("rows1_used")
        hid_done = sem("hid_done")
        logit_ready = sem("logit_ready")
        sig_ready = sem("sig_ready")
        mask_steps = sem("mask_steps")
        mk_ready = sem("mk_ready")
        rs_ps = sem("rowsum_in_psum")
        rs_added = sem("rowsum_added")
        x_copied = sem("x_copied")
        x_stored = [sem(f"x_stored{g}") for g in range(2)]

        ix2_in = [sem(f"ix2_in{slot}") for slot in range(4)]
        lo_in = [sem(f"lo_in{g}") for g in range(2)]
        xr_in = [sem(f"xr_in{slot}") for slot in range(4)]
        lo_made = sem("lo_onehot_made")
        look_ps = sem("lookup_in_psum")
        pick_made = sem("picked_made")
        dcol_ready = sem("dcol_ready")
        x_scaled = sem("x_scaled")
        rows2_in = [sem(f"rows2_in{slot}") for slot in range(4)]
        sel2_ready = sem("sel2_ready")
        seg_ps = sem("segment_in_psum")
        seg_added = sem("segment_added")
        banks_zero = sem("banks_zero")
        out_ready = sem("out_ready")
        out_done = sem("out_done")

        block = ctx.enter_context(nc.Block())
        view = "p (b c) -> p b c"
        x3, s3, a3, t3 = (a[:].rearrange(view, c=C) for a in (x_cur, stage, acc, total))
        p3 = p_f32.rearrange(view, c=C)
        BLOCK_HALVES = (slice(0, NB // 2), slice(NB // 2, NB))
        HALVES = ((0, 4), (4, CB - 4))

        def tbank(k):
            return banks[k % 2][:].bitcast(BF16)[:, 0:GT * P]

        def weighted_groups(stored):
            return (0, 2, 1, 3) if stored else (0, 1, 2, 3)

        def slot_of(stored, u, k):
            return 2 * u + k if stored else k

        def uses(stored, first, i, i1):
            return first + (i if stored else i1)

        def table(d):
            return d.rearrange("(b p) c -> p b c", p=P)

        @block.sync
        def _(sp):
            def edge_load(to, given):
                sp.dma_start(to[0:LA, :], given[0:LA * T].rearrange("(p t) -> p t", t=T)).then_inc(edges_in, 16)
                sp.dma_start(to[LA:LANES, :], given[LA * T:LANES * T].rearrange("(p t) -> p t", t=T)).then_inc(edges_in, 16)
                sp.dma_start(to[LANES:LANES + 1, 0:TAIL], given[LANES * T:E].rearrange("(p t) -> p t", p=1)).then_inc(edges_in, 16)

            sp.wait_ge(pad_set, 1)
            edge_load(src_i, src)
            edge_load(dst_i, dst)
            sp.wait_ge(pad_set, 2)
            sp.dma_start(sorted_d.rearrange("(p t) o -> p (t o)", t=NT), fill_i).then_inc(fill_out, 16)
            sp.dma_start(x3[:, 0:FULL, :], table(x[0:FULL * P, :])).then_inc(x_in, 16)
            sp.dma_start(x3[0:REST, FULL, :], x[FULL * P:N, :]).then_inc(x_in, 16)
            loads = [
                (wcat_all[:, :, 0:C], nb_W.rearrange("l i o -> i l o")),
                (wcat_all[:, :, C:P], self_W.rearrange("l i o -> i l o")),
                (bd_all[0:C, :, 0:C], att1_W[:, 0:C, :].rearrange("l i o -> i l o")),
                (bd_all[C:P, :, C:P], att1_W[:, C:P, :].rearrange("l i o -> i l o")),
                (a1b_all[:].rearrange("p l c -> p (l c)"), att1_b.rearrange("l c -> (l c)").partition_broadcast(P)),
                (a2w_all[:].rearrange("p l c -> p (l c)"), att2_W.rearrange("l c o -> (l c o)").partition_broadcast(P)),
                (a2b_all[:], att2_b.rearrange("l o -> (l o)").partition_broadcast(P)),
                (w1[:], l1_W),
                (b1[:], l1_b.partition_broadcast(P)),
            ]
            for to, given in loads:
                sp.dma_start(to, given).then_inc(weights_in, 16)
            for l in range(L):
                sp.dma_start(bcat_all[0:C, l:l + 1], nb_b[l].rearrange("(c o) -> c o", o=1)).then_inc(weights_in, 16)
                sp.dma_start(bcat_all[C:P, l:l + 1], self_b[l].rearrange("(c o) -> c o", o=1)).then_inc(weights_in, 16)

            sp.wait_ge(counted, 1)
            sp.dma_start(cnt_d.rearrange("s (h l) -> h s l", l=NLO), cnt_small.rearrange("h (s l) -> h s l", l=NLO)
                         ).then_inc(cnt_out, 16)
            sp.wait_ge(cnt_out, 16)
            sp.dma_start(cnt.rearrange("p (s b) -> p s b", b=NB), cnt_d[:, 0:NB].partition_broadcast(P)).then_inc(cnt_in, 16)

            sp.wait_ge(gtab_ready, 1)
            sp.dma_start(gtab_d, gtab_i[:]).then_inc(gtab_out, 16)
            sp.wait_ge(gtab_out, 16)
            sp.dma_start(gblk[0:1, BP:BP + P * GJ], gtab_d.rearrange("(o p) j -> o (p j)", o=1)).then_inc(gblk_in, 16)
            for h in range(2):
                sp.wait_ge(scattered[h], (T // SORT) * 8 * 16)
            sp.dma_start(packed, sorted_d.rearrange("(p t) o -> p (t o)", t=NT)).then_inc(packed_in, 16)
            sp.wait_ge(col_ready, 1)
            sp.dma_start(col_d, col_i).then_inc(col_out, 16)
            sp.wait_ge(hi_ready, 1)
            sp.dma_start(hi_d, hi).then_inc(hi_out, 16)
            sp.wait_ge(hi_out, 16)
            sp.wait_ge(loT_ready, LO_CHUNKS)
            lo_tiles = lo_d.rearrange("(t p) -> t p", p=P)
            if NT // P:
                sp.dma_start(lo_tiles[0:NT // P * P, :].rearrange("(c t) p -> t c p", t=P),
                             loT[:, 0:NT // P * P].rearrange("t (c p) -> t c p", p=P)).then_inc(lo_out, 16)
            if NT % P:
                sp.dma_start(lo_tiles[NT // P * P:NT, :], loT[0:NT % P, NT // P * P:(NT // P + 1) * P]).then_inc(lo_out, 16)
            sp.wait_ge(lo_out, 16 * LO_OUTS)
            sp.wait_ge(col_out, 16)

            sp.wait_ge(ctl_ready, 1)
            n_it = sp.value_load(ctl[0:1, 0:1], min_val=2, max_val=NI_MAX)
            n_two = sp.value_load(ctl[0:1, 1:2], min_val=1, max_val=NI_MAX // 2)

            def index_loads1(first):
                with sp.Fori(0, n_it) as i:
                    it = sp.snap(first + i)
                    for h in range(2):
                        sp.wait_ge(rows1_in[2 * h], it * 64)
                        sp.wait_ge(rows1_in[2 * h + 1], it * 64)
                        sp.dma_start(ix[:, 8 * h:8 * h + 8], col_d[:, bass.ds(i * BT + 8 * h, 8)]).then_inc(ix1_in[h], 16)

            def lo_load(l, i, g):
                wait_alone(sp, lo_made, l * (n_it + 1) * 2 + i * 2 + g + 1)
                sp.dma_start(lo_row[:, g, :], lo_d[bass.ds((i * BT + (g + 2) * GT) * P, GT * P)].partition_broadcast(P)
                             ).then_inc(lo_in[g], 16)

            def loads2(l, stored):
                with sp.Fori(0, n_two) as i:
                    for u in range(2):
                        i1 = sp.snap(i * 2 + u)
                        it = sp.snap(l * n_it + i1)
                        if stored:
                            for g in range(2):
                                lo_load(l, i1, g)
                        for s, k in enumerate(weighted_groups(stored)):
                            if stored and k >= 2:
                                wait_alone(sp, seg_ps, it * BG + s + 1)
                                sp.dma_start(x_slots[:, 2 * u + k - 2, :], xg_d[:, bass.ds((i1 * 2 + k - 2) * GT * C, GT * C)]
                                             ).then_inc(xr_in[2 * u + k - 2], 16)
                            else:
                                slot = slot_of(stored, u, k)
                                wait_alone(sp, rows2_in[slot], uses(stored, l * n_two, i, i1) * 64)
                                sp.dma_start(ix[:, GT * slot:GT * (slot + 1)], col_d[:, bass.ds(i1 * BT + GT * k, GT)]
                                             ).then_inc(ix2_in[slot], 16)
                if stored:
                    for g in range(2):
                        wait_alone(sp, lo_made, (l * (n_it + 1) + n_it) * 2 + g + 1)
                        sp.dma_start(lo_row[:, g, :], lo_d[(g + 2) * GT * P:(g + 3) * GT * P].partition_broadcast(P)
                                     ).then_inc(lo_in[g], 16)

            def xd_stores(l):
                for h, half in enumerate(BLOCK_HALVES):
                    sp.wait_ge(xd_ready, l * 2 + h + 1)
                    sp.dma_start(table(xd_d)[:, half, :], s3[:, half, :]).then_inc(xd_out, 16)

            with sp.Fori(0, L) as l:
                for slot in range(4):
                    wait_alone(sp, rows2_in[slot], l * n_two * 64)
                sp.wait_ge(layer_w, l + 1)
                sp.dma_start(table(qx_d[:, C:2 * C]), x3).then_inc(q_out, 16)
                with sp.Fori(0, NCH // 2) as j:
                    sp.wait_ge(pq_read, (l * NCH + j * 2) * 2 + 6)
                    blocks = bass.ds(j * (2 * CB), 2 * CB)
                    sp.dma_start(table(q_d)[:, blocks, :], s3[:, blocks, :]).then_inc(q_out, 16)
                    sp.dma_start(table(qx_d[:, 0:C])[:, blocks, :], s3[:, blocks, :]).then_inc(q_out, 16)
                index_loads1(l * n_it)
                for k in range(BG):
                    sp.wait_ge(rows1_in[k], (l + 1) * n_it * 64)
                xd_stores(l)
                sp.dma_start(hi, hi_d).then_inc(hi_in, 16)
                loads2(l, True)
            xd_stores(L)
            loads2(L, False)

            sp.wait_ge(out_ready, 1)
            sp.dma_start(table(out[0:FULL * P, :]), a3[:, 0:FULL, :]).then_inc(out_done, 16)
            sp.dma_start(out[FULL * P:N, :], a3[0:REST, FULL, :]).then_inc(out_done, 16)
            sp.wait_ge(out_done, 32)

        @block.gpsimd
        def _(pool):
            nc.gpsimd.memset(ones_bf[:], 1.0)
            nc.gpsimd.memset(ident[:], 1.0)
            for d in range(3):
                nc.gpsimd.memset(digits_w[:, d, :], float(256 ** d))
            nc.gpsimd.memset(mk[:], 1.0).then_inc(ones_ready, 1)
            nc.gpsimd.iota(iota_bf[:], [[1, P]], base=0, channel_multiplier=0, allow_small_or_imprecise_dtypes=True)
            nc.gpsimd.iota(iota_p[:], [[1, 1]], base=0, channel_multiplier=1, allow_small_or_imprecise_dtypes=True)
            nc.gpsimd.iota(iota_n[:], [[1, P]], base=0, channel_multiplier=0, allow_small_or_imprecise_dtypes=True)
            nc.gpsimd.iota(gval[:], [[1, GJ]], base=0, channel_multiplier=GJ, allow_small_or_imprecise_dtypes=True)
            pool.wait_ge(ones_ready, 1)
            nc.gpsimd.affine_select(out=before[:], in_=ones_bf[:], pattern=[[1, P]], compare_op=ALU.is_gt,
                                    fill=0.0, base=0, channel_multiplier=-1)
            nc.gpsimd.affine_select(out=notbefore[:], in_=ones_bf[:], pattern=[[-1, P]], compare_op=ALU.is_ge,
                                    fill=0.0, base=0, channel_multiplier=1)
            nc.gpsimd.affine_select(out=ident_bf[:], in_=ones_bf[:], pattern=[[-1, P]], compare_op=ALU.is_equal,
                                    fill=0.0, base=0, channel_multiplier=1)
            nc.gpsimd.affine_select(out=ident[:], in_=ident[:], pattern=[[-1, P]], compare_op=ALU.is_equal,
                                    fill=0.0, base=0, channel_multiplier=1).then_inc(const_ready, 1)

            pool.wait_ge(fill_out, 16)
            with pool.Fori(0, T // SORT) as i:
                for h in range(2):
                    wait_alone(pool, adr_ready[h], i + 1)
                    for j in range(8):
                        nc.gpsimd.indirect_dma_start(
                            out=sorted_d, out_offset=bass.IndirectOffsetOnAxis(ap=adr[:, h, j:j + 1], axis=0),
                            in_=val[:, h, j:j + 1], in_offset=None).then_inc(scattered[h], 16)

            pool.wait_ge(ctl_ready, 1)
            n_it = pool.value_load(ctl[0:1, 0:1], min_val=2, max_val=NI_MAX)
            n_two = pool.value_load(ctl[0:1, 1:2], min_val=1, max_val=NI_MAX // 2)

            def gather(to, table_d, t, done):
                nc.gpsimd.indirect_dma_start(
                    out=to, out_offset=None, in_=table_d,
                    in_offset=bass.IndirectOffsetOnAxis(ap=ix[:, t:t + 1], axis=0)).then_inc(done, 16)

            def gathers1(first):
                with pool.Fori(0, n_it) as i:
                    it = pool.snap(first + i)
                    for k in range(BG):
                        if k % 2 == 0:
                            pool.wait_ge(ix1_in[k // 2], (it + 1) * 16)
                        wait_alone(pool, rows1_used, it * BG + k + 1)
                        if k >= 2:
                            wait_alone(pool, x_copied, it * 2 + k - 1)
                        for j in range(GT):
                            if k < 2:
                                gather(rows[:, k, j * C:(j + 1) * C], q_d, GT * k + j, rows1_in[k])
                            else:
                                gather(qx_rows[k - 2][:, j * 2 * C:(j + 1) * 2 * C], qx_d, GT * k + j, rows1_in[k])

            def gathers2(l, stored):
                with pool.Fori(0, n_two) as i:
                    for u in range(2):
                        i1 = pool.snap(i * 2 + u)
                        it = pool.snap(l * n_it + i1)
                        for s, k in enumerate(weighted_groups(stored)):
                            if stored and k >= 2:
                                continue
                            slot = slot_of(stored, u, k)
                            pool.wait_ge(ix2_in[slot], (uses(stored, l * n_two, i, i1) + 1) * 16)
                            wait_alone(pool, seg_ps, it * BG + s + (1 if stored else 1 + BG))
                            for j in range(GT):
                                gather(rows[:, slot, j * C:(j + 1) * C], xd_d, GT * slot + j, rows2_in[slot])

            with pool.Fori(0, L) as l:
                wait_alone(pool, layer_w, l + 1)
                with pool.Fori(0, NCH // 2) as j:
                    c0 = pool.snap(j * 2)
                    H = pool.snap((l * NCH + c0) * 2)
                    for s in range(2):
                        pool.wait_ge(xT_ps, H + 2 * s)
                        nc.gpsimd.tensor_copy(xs[:, s, :], x_cur[:, bass.ds((c0 + s) * (CB * C), CB * C)]).then_inc(xs_ready, 1)
                wait_alone(pool, q_out, (l + 1) * Q_STORES * 16)
                gathers1(l * n_it)
                wait_alone(pool, xd_out, (l + 1) * 32)
                gathers2(l, True)
            pool.wait_ge(xd_out, (L + 1) * 32)
            gathers2(L, False)

        @block.scalar
        def _(act):
            act.wait_ge(ctl_ready, 1)
            n_it = act.value_load(ctl[0:1, 0:1], min_val=2, max_val=NI_MAX)
            n_two = act.value_load(ctl[0:1, 1:2], min_val=1, max_val=NI_MAX // 2)
            act.sem_inc(selT_ready, 2)
            act.sem_inc(x_copied, 2)
            act.sem_inc(dcol_ready, 2)
            act.sem_inc(x_scaled, 2)
            for c in range(LO_CHUNKS):
                n = min(P, NT - c * P)
                act.wait_ge(loT_ps, c + 1)
                nc.scalar.copy(loT[0:n, c * P:(c + 1) * P], banks[c % 2][0:n, 0:P]).then_inc(loT_ready, 1)
            act.sem_inc(xT_ready, 2)
            act.sem_inc(f_ready, 2)

            def x_transposed(H, h):
                first, n = HALVES[h]
                act.wait_ge(xT_ps, H + h + 3)
                act.wait_ge(f_ps, H + h + 1)
                nc.scalar.copy(xT[:, first * P:(first + n) * P], banks[h][0:C, 0:n * P]).then_inc(xT_ready, 1)

            def root(r):
                act.wait_ge(root_in, r)
                nc.scalar.activation(nodeB[:], nodeA[:], ACT.Sqrt).then_inc(root_done, 1)

            with act.Fori(0, L) as l:
                act.wait_ge(layer_w, l + 1)
                nc.scalar.activation(warm[:], a2b[:], ACT.Sigmoid)
                with act.Fori(0, NCH) as j:
                    H = act.snap((l * NCH + j) * 2)
                    for h in range(2):
                        x_transposed(H, h)
                    for h, (first, n) in enumerate(HALVES):
                        act.wait_ge(f_ps, H + h + 3)
                        act.wait_ge(pq_ps, H + h + 1)
                        nc.scalar.activation(feat[:, first * P:(first + n) * P], banks[2 + h][:, 0:n * P], ACT.Relu,
                                             bias=bcat[:, 0:1]).then_inc(f_ready, 1)
                with act.Fori(0, n_it) as i:
                    it = act.snap(l * n_it + i)
                    for k in range(BG):
                        act.wait_ge(selT_ps, it * BG + k + 1)
                        act.wait_ge(pg_ps, it * BG + k + 1)
                        nc.scalar.copy(selT[:, k % 2, :], tbank(k)).then_inc(selT_ready, 1)
                    for g in range(2):
                        act.wait_ge(rows1_in[2 + g], (it + 1) * 64)
                        act.wait_ge(x_stored[g], it * 16)
                        nc.scalar.copy(x_out_buf[:, g, :].rearrange("p (t c) -> p t c", c=C), x_rows[g]).then_inc(x_copied, 1)
                    for g in range(2):
                        act.wait_ge(x_copied, it * 2 + g + 3)
                        act.dma_start(xg_d[:, bass.ds((i * 2 + g) * GT * C, GT * C)], x_out_buf[:, g, :]).then_inc(x_stored[g], 16)
                    act.wait_ge(logit_ready, (it + 1) * BG)
                    nc.scalar.activation(sig[:], logit[:], ACT.Sigmoid, bias=a2b[:, 0:1]).then_inc(sig_ready, 1)
                for g in range(2):
                    act.wait_ge(x_stored[g], (l + 1) * n_it * 16)
                root(l + 1)
                with act.Fori(0, n_two) as i:
                    for u in range(2):
                        it = act.snap(l * n_it + (i * 2 + u))
                        for g in range(2):
                            act.wait_ge(pick_made, it * 2 + g + 3)
                            act.wait_ge(x_scaled, it * 2 + g + 1)
                            for j in range(GT):
                                one = picked[g][:, j * NB:(j + 1) * NB]
                                ins = nc.scalar.activation(one, one, ACT.Copy, accum_out=dcol[:, g * GT + j:g * GT + j + 1])
                            ins.then_inc(dcol_ready, 1)
                        for g in range(2):
                            slot = 2 * u + g
                            act.wait_ge(dcol_ready, it * 2 + g + 3)
                            act.wait_ge(xr_in[slot], (l * n_two + i + 1) * 16)
                            for j in range(GT):
                                x_tile = x_slots[:, slot, j * C:(j + 1) * C]
                                ins = nc.scalar.activation(x_tile, x_tile, ACT.Copy, scale=dcol[:, g * GT + j:g * GT + j + 1])
                            ins.then_inc(x_scaled, 1)
            for r in range(3):
                root(L + 1 + r)
                if r == 1:
                    with act.Fori(0, NCH) as j:
                        H = act.snap((j + L * NCH) * 2)
                        for h in range(2):
                            x_transposed(H, h)

        @block.tensor
        def _(pe):
            pe.sem_inc(oh_used, 2)
            pe.sem_inc(oh2_used, 4)
            pe.sem_inc(xT_ps, 2)
            pe.sem_inc(f_ps, 2)
            pe.sem_inc(pq_ps, 2)
            pe.sem_inc(pg_ps, 2)
            pe.sem_inc(rs_ps, 1)
            pe.sem_inc(seg_ps, 2 * BG)
            pe.wait_ge(const_ready, 1)
            pe.wait_ge(count_zero, 1)
            with pe.Fori(0, T // (2 * SORT)) as i:
                for a in range(2):
                    pe.wait_ge(oh_ready, i * 2 + a + 1)
                    for t in range(SORT):
                        s = t % NS
                        mm = pe.matmul(banks[0][0:NHI, s * NLO:(s + 1) * NLO], hi_hot[:, a, t * NHI:(t + 1) * NHI],
                                       lo_hot[:, a, t * NLO:(t + 1) * NLO], start=False, stop=False, skip_group_check=True)
                    mm.then_inc(oh_used, 1)
            pe.wait_ge(base_ready, 1)
            for c in range(2):
                for d in range(3):
                    pe.matmul(banks[2 + c][:, 0:4 * NB], digits_w[0:1, d, :],
                              digits[d][:, c * 4 * NB:(c + 1) * 4 * NB], start=(d == 0), stop=False,
                              skip_group_check=True)
            with pe.Fori(0, T // SORT) as i:
                for c in range(4):
                    bank = banks[2 + c % 2]
                    pe.wait_ge(oh2_ready, i * 4 + c + 1)
                    pe.matmul(bank[:, 0:4 * NB], before[:], onehot[:, c, :], start=False, stop=False,
                              skip_group_check=True).then_inc(rank_ready, 1)
                    pe.wait_ge(rank_read, i * 4 + c + 1)
                    pe.matmul(bank[:, 0:4 * NB], notbefore[:], onehot[:, c, :], start=False, stop=False,
                              skip_group_check=True).then_inc(oh2_used, 1)

            pe.wait_ge(ctl_ready, 1)
            pe.wait_ge(gblk_in, 16)
            n_it = pe.value_load(ctl[0:1, 0:1], min_val=2, max_val=NI_MAX)
            n_two = pe.value_load(ctl[0:1, 1:2], min_val=1, max_val=NI_MAX // 2)
            blk_regs = [pe.alloc_register(f"pe_blk{q}") for q in range(BP)]
            pe.wait_ge(lo_ready, 1)
            for c in range(LO_CHUNKS):
                n = min(P, NT - c * P)
                if c >= 2:
                    pe.wait_ge(loT_ready, c - 1)
                pe.transpose(banks[c % 2][0:n, 0:P], lo_f[:, c * P:c * P + n], ident[:]).then_inc(loT_ps, 1)
            pe.wait_ge(loT_ready, LO_CHUNKS)

            def transpose_x(H, s):
                wait_alone(pe, xs_ready, H // 2 + 1)
                for h, (first, n) in enumerate(HALVES):
                    wait_alone(pe, xT_ready, H + h + 1)
                    for b in range(n):
                        mm = pe.transpose(banks[h][0:C, b * P:(b + 1) * P],
                                          xs[:, s, (first + b) * C:(first + b + 1) * C], ident[:])
                    mm.then_inc(xT_ps, 1)

            def lookups(turn, picks):
                for g in range(2):
                    pe.wait_ge(lo_made, turn * 2 + g + 3)
                    pe.wait_ge(pick_made, picks * 2 + g + 1)
                    for j in range(GT):
                        for pl in range(NPL):
                            mm = pe.matmul(banks[2 + g][:, j * NB:(j + 1) * NB], lo_onehot[:, g, j * P:(j + 1) * P],
                                           dinv_pl[:, pl * NB:(pl + 1) * NB], start=(pl == 0), stop=(pl == NPL - 1))
                    mm.then_inc(look_ps, 1)

            def segment_sums(l, stored):
                if stored:
                    lookups(l * (n_it + 1), l * n_it)
                with pe.Fori(0, n_two) as i:
                    for u in range(2):
                        i1 = pe.snap(i * 2 + u)
                        it = pe.snap(l * n_it + i1)
                        A0 = pe.snap((it + l) * BG * 2)
                        for s, k in enumerate(weighted_groups(stored)):
                            if stored and s == 2:
                                lookups(it + l + 1, it + 1)
                            pe.wait_ge(sel2_ready, it * BG + s + 1)
                            pe.wait_ge(seg_added, A0 + 2 * s + 3)
                            if stored and k >= 2:
                                pe.wait_ge(x_scaled, it * 2 + k + 1)
                                given = x_slots[:, 2 * u + k - 2, :]
                            else:
                                slot = slot_of(stored, u, k)
                                pe.wait_ge(rows2_in[slot], (uses(stored, l * n_two, i, i1) + 1) * 64)
                                given = rows[:, slot, :]
                            for j in range(GT):
                                q = j // PT
                                mm = pe.matmul(seg_banks[s][:, q * C:(q + 1) * C], wsel[:, s, j * P:(j + 1) * P],
                                               given[:, j * C:(j + 1) * C], start=(j % PT == 0), stop=(j % PT == PT - 1))
                            mm.then_inc(seg_ps, 1)

            with pe.Fori(0, L) as l:
                wait_alone(pe, layer_w, l + 1)

                def features(H):
                    for h, (first, n) in enumerate(HALVES):
                        pe.wait_ge(xT_ready, H + h + 3)
                        pe.wait_ge(f_ready, H + h + 1)
                        pe.matmul(banks[2 + h][:, 0:n * P], wcat[:], xT[:, first * P:(first + n) * P],
                                  start=True, stop=True).then_inc(f_ps, 1)

                def halves_of_hidden(H):
                    for h, (first, n) in enumerate(HALVES):
                        pe.wait_ge(f_ready, H + h + 3)
                        pe.wait_ge(pq_read, H + h + 1)
                        for b in range(n):
                            mm = pe.matmul(banks[4 + h][:, b * P:(b + 1) * P], feat[:, (first + b) * P:(first + b + 1) * P],
                                           bd[:], start=True, stop=True)
                        mm.then_inc(pq_ps, 1)

                with pe.Fori(0, NCH // 2) as j:
                    H = pe.snap((l * NCH + j * 2) * 2)
                    transpose_x(H, 0)
                    features(H)
                    transpose_x(H + 2, 1)
                    halves_of_hidden(H)
                    features(H + 2)
                    halves_of_hidden(H + 2)
                with pe.Fori(0, n_it) as i:
                    it = pe.snap(l * n_it + i)
                    G0 = pe.snap(it * BG)
                    pe.load(blk_regs, gblk[0:1, bass.ds((i + 1) * BP, BP)])
                    blks = [pe.snap(r, min_val=0, max_val=NB - 1) for r in blk_regs]
                    for k in range(BG):
                        pe.wait_ge(sel_ready, G0 + k + 1)
                        pe.wait_ge(selT_ready, G0 + k + 1)
                        for j in range(GT):
                            mm = pe.transpose(tbank(k)[:, j * P:(j + 1) * P], sel[:, k, j * P:(j + 1) * P], ident_bf[:])
                        mm.then_inc(selT_ps, 1)
                        pe.wait_ge(selT_ready, G0 + k + 3)
                        pe.wait_ge(rows1_used, G0 + k + 3)
                        for j in range(GT):
                            b = blks[(k * GT + j) // PT]
                            for pl in range(NPL):
                                mm = pe.matmul(banks[2 + k % 2][:, j * C:(j + 1) * C], selT[:, k % 2, j * P:(j + 1) * P],
                                               p_node[:, bass.ds(b * (NPL * C) + pl * C, C)],
                                               start=(pl == 0), stop=(pl == NPL - 1))
                        mm.then_inc(pg_ps, 1)
                    pe.wait_ge(mk_ready, it + 1)
                    pe.wait_ge(rs_added, it * BP + 1)
                    for t in range(BT):
                        q = t // PT
                        mm = pe.matmul(banks[4][:, q * (NPL + 1):(q + 1) * (NPL + 1)],
                                       sel[:, t // GT, t % GT * P:(t % GT + 1) * P], mk[:, t, :],
                                       start=(t % PT == 0), stop=(t % PT == PT - 1))
                    mm.then_inc(rs_ps, 1)
                segment_sums(l, True)
            segment_sums(L, False)
            with pe.Fori(0, NCH // 2) as j:
                H = pe.snap((j * 2 + L * NCH) * 2)
                for s in range(2):
                    transpose_x(H + 2 * s, s)
                    for h, (first, n) in enumerate(HALVES):
                        pe.wait_ge(xT_ready, H + 2 * s + h + 3)
                        pe.wait_ge(pq_read, H + 2 * s + h + 1)
                        for b in range(n):
                            mm = pe.matmul(banks[2 + h][:, b * C:(b + 1) * C], xT[:, (first + b) * P:(first + b + 1) * P],
                                           w1[:], start=True, stop=True)
                        mm.then_inc(f_ps, 1)

        @block.vector
        def _(dve):
            v = nc.vector
            pad_lane = (LANES // 32) * 32
            v.memset(src_i[pad_lane:P, :], float(NP - 1))
            v.memset(dst_i[pad_lane:P, :], 0.0).then_inc(pad_set, 1)
            v.memset(fill_i, float(PAD))
            v.memset(x3[:, FULL:NB, :], 0.0)
            v.memset(bd_all[:], 0.0).then_inc(pad_set, 1)
            v.memset(banks[0][0:NHI, 0:NS * NLO], 0.0).then_inc(count_zero, 1)
            for s, n in ((pq_read, 2), (rows1_used, 4), (rs_added, 1), (seg_added, 1), (lo_made, 2),
                         (pick_made, 2)):
                dve.sem_inc(s, n)

            st = Steps(sv)
            dve.wait_ge(edges_in, 96)
            v.tensor_scalar(blk_i, src_i, 7, None, ALU.logical_shift_right)
            st.done(v.tensor_scalar(src_i, src_i, P - 1, None, ALU.bitwise_and))
            st.wait(dve)
            st.done(v.scalar_tensor_tensor(val_i, dst_i, 256.0, src_i, ALU.mult, ALU.add))
            st.wait(dve)
            dve.wait_ge(const_ready, 1)
            st.done(v.tensor_scalar(bhi_i, blk_i, 3, None, ALU.logical_shift_right))
            st.done(v.tensor_scalar(blo_i, blk_i, NLO - 1, None, ALU.bitwise_and))
            st.wait(dve)

            def one_hot(i, c):
                keys = blk_i[:, bass.ds(i * SORT + 4 * c, 4)].unsqueeze(2).to_broadcast([P, 4, NB])
                ids = iota_bf[:, 0:NB].unsqueeze(1).to_broadcast([P, 4, NB])
                return v.tensor_tensor(onehot[:, c, :].rearrange("p (t b) -> p t b", b=NB), keys, ids, ALU.is_equal)

            with dve.Fori(0, T // (2 * SORT)) as i:
                for a in range(2):
                    dve.wait_ge(oh_used, i * 2 + a + 1)
                    for hots, digit, n in ((hi_hot, bhi_i, NHI), (lo_hot, blo_i, NLO)):
                        ins = v.tensor_tensor(hots[:, a, :].rearrange("p (t b) -> p t b", b=n),
                                              digit[:, bass.ds((i * 2 + a) * SORT, SORT)].unsqueeze(2).to_broadcast([P, SORT, n]),
                                              iota_bf[:, 0:n].unsqueeze(1).to_broadcast([P, SORT, n]), ALU.is_equal)
                    ins.then_inc(oh_ready, 1)

            dve.wait_ge(oh_used, 2 + T // SORT)
            v.tensor_copy(cnt_small, banks[0][0:NHI, 0:NS * NLO]).then_inc(counted, 1)
            dve.wait_ge(cnt_in, 16)
            st.done(v.tensor_reduce(tot, cnt.rearrange("p (s b) -> p b s", b=NB), AX_X, ALU.add))
            st.wait(dve)
            st.done(v.tensor_scalar(grp_i, tot, float(PAIR - 1), None, ALU.add))
            st.wait(dve)
            st.done(v.tensor_scalar(grp_i, grp_i, 8, None, ALU.logical_shift_right))
            st.wait(dve)
            st.done(v.tensor_copy(grp, grp_i))
            st.done(v.memset(tot, 1.0))
            st.wait(dve)
            st.done(v.tensor_tensor_scan(gcum, tot, grp, 0.0, ALU.mult, ALU.add))
            st.wait(dve)
            st.done(v.tensor_scalar(ctl[0:1, 2:3], gcum[0:1, NB - 1:NB], float(2 * BP - 1), None, ALU.add))
            st.done(v.tensor_tensor(grp, gcum, grp, ALU.subtract))
            st.wait(dve)
            v.tensor_scalar(ctl[0:1, 0:1], ctl[0:1, 2:3], 4, 1, ALU.logical_shift_right, ALU.logical_shift_left)
            v.tensor_scalar(ctl[0:1, 1:2], ctl[0:1, 2:3], 4, None, ALU.logical_shift_right).then_inc(ctl_ready, 1)
            st.done(v.tensor_scalar(base[:, 0:NB], grp, float(PAIR), None, ALU.mult))
            for s in range(1, NS):
                st.wait(dve)
                st.done(v.tensor_tensor(base[:, s * NB:(s + 1) * NB], base[:, (s - 1) * NB:s * NB],
                                        cnt[:, (s - 1) * NB:s * NB], ALU.add))
            st.wait(dve)
            st.done(v.tensor_copy(base_i[0:1, :], base[0:1, :]))
            st.wait(dve)
            for d in range(3):
                st.done(v.tensor_scalar(digit_i[0:1, :], base_i[0:1, :], 8 * d, 255, ALU.logical_shift_right, ALU.bitwise_and))
                st.wait(dve)
                st.done(v.tensor_copy(digits[d], digit_i[0:1, :]))
                st.wait(dve)
            dve.sem_inc(base_ready, 1)
            cmp3 = cmp_g.rearrange("p (j b) -> p j b", b=NB - 1)
            st.done(v.tensor_tensor(cmp3, gval[:].unsqueeze(2).to_broadcast([P, GJ, NB - 1]),
                                    gcum[:, 0:NB - 1].unsqueeze(1).to_broadcast([P, GJ, NB - 1]), ALU.is_ge))
            st.wait(dve)
            st.done(v.tensor_reduce(gtab[:], cmp3, AX_X, ALU.add))
            st.wait(dve)
            v.memset(gblk[0:1, 0:BP], 0)
            v.tensor_copy(gtab_i[:], gtab[:]).then_inc(gtab_ready, 1)

            ADR = 2 * 5
            with dve.Fori(0, T // SORT) as i:
                ad = Steps(adr_steps, i * ADR)
                for h in range(2):
                    for c in (2 * h, 2 * h + 1):
                        dve.wait_ge(oh2_used, i * 4 + c + 1)
                        one_hot(i, c).then_inc(oh2_ready, 1)
                        dve.wait_ge(rank_ready, i * 4 + c + 1)
                        dve.wait_ge(oh2_ready, i * 4 + c + 1)
                        v.tensor_tensor(prod, banks[2 + c % 2][:, 0:4 * NB], onehot[:, c, :], ALU.mult).then_inc(rank_read, 1)
                        dve.wait_ge(rank_read, i * 4 + c + 1)
                        ad.done(v.tensor_reduce(posf[:, h, 4 * (c % 2):4 * (c % 2) + 4],
                                                prod.rearrange("p (t b) -> p t b", b=NB), AX_X, ALU.add))
                    ad.wait(dve)
                    pos, lane, tile, sub = (adr_w[:, w, :] for w in range(4))
                    ad.done(v.tensor_copy(pos, posf[:, h, :]))
                    ad.wait(dve)
                    v.tensor_scalar(lane, pos, 1, P - 1, ALU.logical_shift_right, ALU.bitwise_and)
                    v.tensor_scalar(tile, pos, 8, 1, ALU.logical_shift_right, ALU.logical_shift_left)
                    ad.done(v.tensor_scalar(sub, pos, PT - 1, None, ALU.bitwise_and))
                    wait_alone(dve, adr_steps, ad.base + ad.n)
                    ad.done(v.tensor_tensor(tile, tile, sub, ALU.add))
                    ad.wait(dve)
                    dve.wait_ge(scattered[h], i * 128)
                    v.scalar_tensor_tensor(adr[:, h, :], lane, float(NT), tile, ALU.mult, ALU.add)
                    v.tensor_copy(val[:, h, :], val_i[:, bass.ds(i * SORT + 8 * h, 8)]).then_inc(adr_ready[h], 1)
                assert ad.n == ADR

            st = Steps(sv, st.n)
            dve.wait_ge(packed_in, 16)
            v.tensor_scalar(col_i, packed, 8, None, ALU.logical_shift_right).then_inc(col_ready, 1)
            st.done(v.tensor_scalar(low_i, packed, PAD, None, ALU.bitwise_and))
            st.wait(dve)
            st.done(v.tensor_copy(rowloc[:], low_i))
            st.wait(dve)
            st.done(v.tensor_scalar(low_i, packed, 8, P - 1, ALU.logical_shift_right, ALU.bitwise_and))
            st.wait(dve)
            st.done(v.tensor_copy(lo_f, low_i))
            st.wait(dve)
            dve.sem_inc(lo_ready, 1)
            hi_i = low_i[:, 0:NT // 2]
            st.done(v.tensor_scalar(hi_i.rearrange("p (i t) -> p i t", t=BT // 2),
                                    packed.rearrange("p (i t) -> p i t", t=BT)[:, :, BT // 2:BT], 15, None,
                                    ALU.logical_shift_right))
            st.wait(dve)
            v.tensor_copy(hi, hi_i).then_inc(hi_ready, 1)
            dve.wait_ge(hi_out, 16)
            dve.wait_ge(loT_ps, LO_CHUNKS)
            dve.wait_ge(lo_out, 16 * LO_OUTS)
            dve.wait_ge(x_in, 32)
            st.done(v.tensor_copy(total[:], x_cur[:]))
            dve.wait_ge(weights_in, (9 + 2 * L) * 16)
            dve.wait_ge(col_out, 16)
            dve.wait_ge(gblk_in, 16)
            n_it = dve.value_load(ctl[0:1, 0:1], min_val=2, max_val=NI_MAX)
            n_two = dve.value_load(ctl[0:1, 1:2], min_val=1, max_val=NI_MAX // 2)
            blk_regs = [dve.alloc_register(f"dve_blk{q}") for q in range(2 * BP)]
            st.wait(dve)

            def per_node(a):
                return a.unsqueeze(2).to_broadcast([P, NB, C])

            def make_xd():
                for half in BLOCK_HALVES:
                    v.tensor_tensor(s3[:, half, :], x3[:, half, :], dinv[:, half].unsqueeze(2).to_broadcast([P, NB // 2, C]),
                                    ALU.mult).then_inc(xd_ready, 1)

            def make_lo_onehot(turn, g):
                dve.wait_ge(lo_in[g], (turn + 1) * 16)
                v.tensor_scalar(lo_onehot[:, g, :], lo_row[:, g, :], iota_p[:, 0:1], None, ALU.is_equal).then_inc(lo_made, 1)

            def segment_adds(l, stored):
                order = weighted_groups(stored)
                for bank in seg_banks:
                    ins = v.memset(bank[:, 0:PT * C], 0.0)
                ins.then_inc(banks_zero, 1)
                dve.wait_ge(banks_zero, l + 1)
                if stored:
                    dve.wait_ge(hi_in, (l + 1) * 16)
                    for g in range(2):
                        make_lo_onehot(l * (n_it + 1), g)

                def add(it, A0, blks, s, q):
                    if q == 0:
                        dve.wait_ge(seg_ps, it * BG + s + 5)
                    dve.wait_ge(seg_added, A0 + 2 * s + q + 1)
                    at = acc[:, bass.ds(blks[2 * order[s] + q] * C, C)]
                    v.tensor_tensor(at, at, seg_banks[s][:, q * C:(q + 1) * C], ALU.add).then_inc(seg_added, 1)

                with dve.Fori(0, n_two) as i:
                    dve.load(blk_regs, gblk[0:1, bass.ds(i * (2 * BP), 2 * BP)])
                    all_blks = [dve.snap(r, min_val=0, max_val=NB - 1) for r in blk_regs]
                    for u in range(2):
                        i1 = dve.snap(i * 2 + u)
                        it = dve.snap(l * n_it + i1)
                        A0 = dve.snap((it + l) * BG * 2)
                        blks = all_blks[u * BP:(u + 1) * BP]

                        def weighted_sel(s, tiles=range(GT)):
                            k = order[s]
                            for j in tiles:
                                t = i1 * BT + (k * GT + j)
                                if j == 0:
                                    dve.wait_ge(seg_ps, it * BG + s + 5)
                                ins = v.tensor_scalar(wsel[:, s, j * P:(j + 1) * P], iota_bf[:], rowloc[:, bass.ds(t, 1)],
                                                      mask_all[:, bass.ds(t, 1)], ALU.is_equal, ALU.mult)
                                if j == GT - 1:
                                    ins.then_inc(sel2_ready, 1)

                        def pick(g):
                            dve.wait_ge(look_ps, (it + l) * 2 + g + 1)
                            dve.wait_ge(dcol_ready, it * 2 + g + 1)
                            for j in range(GT):
                                ins = v.scalar_tensor_tensor(picked[g][:, j * NB:(j + 1) * NB], iota_bf[:, 0:NB],
                                                             hi[:, bass.ds((i1 * 2 + g) * GT + j, 1)],
                                                             banks[2 + g][:, j * NB:(j + 1) * NB], ALU.is_equal, ALU.mult)
                            ins.then_inc(pick_made, 1)

                        if stored:
                            weighted_sel(0, (0, 1))
                            add(it, A0, blks, 0, 0)
                            weighted_sel(0, (2, 3))
                            add(it, A0, blks, 0, 1)
                            pick(0)
                            add(it, A0, blks, 1, 0)
                            pick(1)
                            add(it, A0, blks, 1, 1)
                            for g in range(2):
                                make_lo_onehot(it + l + 1, g)
                            weighted_sel(1)
                        else:
                            weighted_sel(0)
                            add(it, A0, blks, 0, 0)
                            weighted_sel(1, (0, 1))
                            add(it, A0, blks, 0, 1)
                            weighted_sel(1, (2, 3))
                            add(it, A0, blks, 1, 0)
                            weighted_sel(2, (0, 1))
                            add(it, A0, blks, 1, 1)
                        weighted_sel(2, (0, 1, 2, 3) if stored else (2, 3))
                        add(it, A0, blks, 2, 0)
                        weighted_sel(3, (0,))
                        add(it, A0, blks, 2, 1)
                        weighted_sel(3, (1,))
                        add(it, A0, blks, 3, 0)
                        weighted_sel(3, (2,))
                        add(it, A0, blks, 3, 1)
                        weighted_sel(3, (3,))
                dve.load(blk_regs[0:BP], gblk[0:1, bass.ds(n_it * BP, BP)])
                blks = [dve.snap(r, min_val=0, max_val=NB - 1) for r in blk_regs[0:BP]]
                it = dve.snap((l + 1) * n_it)
                A0 = dve.snap((it + l) * BG * 2)
                for s in range(BG):
                    for q in range(2):
                        add(it, A0, blks, s, q)

            NODE_STEPS = 24
            with dve.Fori(0, L) as l:
                ns = Steps(nv, l * NODE_STEPS)
                for to, given in ((wcat[:], wcat_all[:, bass.ds(l, 1), :]), (bd[:], bd_all[:, bass.ds(l, 1), :]),
                                  (bcat[:], bcat_all[:, bass.ds(l, 1)]), (a1b[:], a1b_all[:, bass.ds(l, 1), :]),
                                  (a2w[:], a2w_all[:, bass.ds(l, 1), :])):
                    if len(given.shape) == 3:
                        given = given.rearrange("p o c -> p (o c)")
                    v.tensor_copy(to, given)
                v.tensor_copy(a2b[:], a2b_all[:, bass.ds(l, 1)]).then_inc(layer_w, 1)
                ns.done(v.memset(rs[:], 0.0))
                ns.wait(dve)
                dve.wait_ge(layer_w, l + 1)
                wait_alone(dve, xd_out, l * 32)

                with dve.Fori(0, NCH // 2) as j:
                    c0 = dve.snap(j * 2)
                    H = dve.snap((l * NCH + c0) * 2)
                    for s in range(2):
                        for h, (first, n) in enumerate(HALVES):
                            dve.wait_ge(pq_ps, H + 2 * s + h + 3)
                            both = banks[4 + h][:, 0:n * P].rearrange("p (b c) -> p b c", c=P)
                            v.tensor_tensor(pf[:, s, first * C:(first + n) * C].rearrange(view, c=C), both[:, :, 0:C],
                                            a1b[:].unsqueeze(1).to_broadcast([P, n, C]), ALU.add)
                            v.tensor_copy(stage[:, bass.ds((c0 + s) * (CB * C) + first * C, n * C)].rearrange(view, c=C),
                                          both[:, :, C:P]).then_inc(pq_read, 1)
                        dve.wait_ge(pq_read, H + 2 * s + 4)
                        planes = p_node[:, bass.ds((c0 + s) * (CB * NPL * C), CB * NPL * C)].rearrange(
                            "p (b l c) -> p b l c", l=NPL, c=C)
                        whole = pf[:, s, :].rearrange(view, c=C)
                        pstep = Steps(plane_steps, H * 2 + 4 * s)
                        for pl in range(NPL - 1):
                            pstep.done(v.tensor_copy(planes[:, :, pl, :], whole))
                            pstep.wait(dve)
                            if pl < NPL - 2:
                                pstep.done(v.tensor_tensor(whole, whole, planes[:, :, pl, :], ALU.subtract))
                                pstep.wait(dve)
                        pstep.done(v.tensor_tensor(planes[:, :, NPL - 1, :], whole, planes[:, :, NPL - 2, :], ALU.subtract))
                dve.wait_ge(plane_steps, (l + 1) * NCH * 4)
                ns.done(v.tensor_tensor(total[:], total[:], x_cur[:], ALU.add))
                ns.done(v.memset(acc[:], 0.0))
                wait_alone(dve, nv, ns.base + ns.n)

                with dve.Fori(0, n_it) as i:
                    it = dve.snap(l * n_it + i)
                    G0 = dve.snap(it * BG)
                    dve.load(blk_regs[0:BP], gblk[0:1, bass.ds((i + 1) * BP, BP)])
                    blks = [dve.snap(r, min_val=0, max_val=NB - 1) for r in blk_regs[0:BP]]
                    dve.wait_ge(rs_ps, it + 1)

                    def plain_sel(k):
                        v.tensor_tensor(sel[:, k, :].rearrange("p (t n) -> p t n", n=P),
                                        iota_n[:].unsqueeze(1).to_broadcast([P, GT, P]),
                                        rowloc[:, bass.ds(i * BT + k * GT, GT)].unsqueeze(2).to_broadcast([P, GT, P]),
                                        ALU.is_equal).then_inc(sel_ready, 1)

                    def tiles(a):
                        return a.rearrange("p (t c) -> p t c", c=C)

                    plain_sel(0)
                    plain_sel(1)
                    for k in range(BG):
                        s = k % 2
                        dve.wait_ge(pg_ps, G0 + k + 3)
                        dve.wait_ge(rows1_in[k], (it + 1) * 64)
                        v.tensor_tensor(tiles(hid[:, s, :]), tiles(banks[2 + s][:, 0:GT * C]), q_rows[k], ALU.add).then_inc(rows1_used, 1)
                        dve.wait_ge(rows1_used, G0 + k + 5)
                        v.scalar_tensor_tensor(tiles(hid2[:, s, :]), tiles(hid[:, s, :]), 0.0,
                                               a2w[:].unsqueeze(1).to_broadcast([P, GT, C]),
                                               ALU.max, ALU.mult).then_inc(hid_done, 1)
                        if k + 2 < BG:
                            plain_sel(k + 2)
                        dve.wait_ge(hid_done, G0 + k + 1)
                        v.tensor_reduce(logit[:, k * GT:(k + 1) * GT], tiles(hid2[:, s, :]), AX_X,
                                        ALU.add).then_inc(logit_ready, 1)
                    ms = Steps(mask_steps, it * 4)
                    mask = mask_all[:, bass.ds(i * BT, BT)]
                    dve.wait_ge(sig_ready, it + 1)
                    ms.done(v.tensor_scalar(stretched[:], sig[:], ZETA - GAMMA, GAMMA, ALU.mult, ALU.add))
                    ms.wait(dve)
                    v.tensor_scalar(mask, stretched[:], 0.0, 1.0, ALU.max, ALU.min)
                    ms.done(v.tensor_scalar(mk[:, :, 0], stretched[:], 0.0, 1.0, ALU.max, ALU.min))
                    ms.wait(dve)
                    ms.done(v.tensor_tensor(mrest[:], mask, mk[:, :, 0], ALU.subtract))
                    ms.wait(dve)
                    ms.done(v.tensor_copy(mk[:, :, 1], mrest[:]))
                    ms.wait(dve)
                    v.tensor_tensor(mk[:, :, 2], mrest[:], mk[:, :, 1], ALU.subtract).then_inc(mk_ready, 1)
                    dve.wait_ge(rs_ps, it + 2)
                    for q in range(BP):
                        dve.wait_ge(rs_added, it * BP + q + 1)
                        at = rs[:, bass.ds(blks[q], 1), :].rearrange("p o c -> p (o c)")
                        v.tensor_tensor(at, at, banks[4][:, q * (NPL + 1):(q + 1) * (NPL + 1)], ALU.add).then_inc(rs_added, 1)

                dve.wait_ge(rs_added, (l + 1) * n_it * BP + 1)
                ns.done(v.tensor_reduce(dinv[:], rs[:, :, 0:NPL], AX_X, ALU.add))
                ns.wait(dve)
                ns.done(v.tensor_scalar(nodeA[:], dinv[:], 1e-6, None, ALU.add))
                ns.wait(dve)
                dve.sem_inc(root_in, 1)
                dve.wait_ge(root_done, l + 1)
                ns.done(v.reciprocal(dinv[:], nodeB[:]))
                ns.wait(dve)
                ns.done(v.tensor_scalar(dinv[:], dinv[:], 10.0, 0.0, ALU.min, ALU.max))
                ns.wait(dve)
                dve.wait_ge(q_out, (l + 1) * Q_STORES * 16)
                make_xd()
                for pl in range(NPL):
                    given = nodeA if pl else dinv
                    plane = dinv_pl[:, pl * NB:(pl + 1) * NB]
                    ns.done(v.tensor_copy(plane, given[:]))
                    ns.wait(dve)
                    if pl < NPL - 1:
                        ns.done(v.tensor_tensor(nodeA[:], given[:], plane, ALU.subtract))
                        ns.wait(dve)
                segment_adds(l, True)
                dve.wait_ge(seg_added, (l + 1) * (n_it + 1) * BP + 1)
                ns.done(v.tensor_tensor(x3, a3, per_node(dinv[:]), ALU.mult))
                ns.wait(dve)
                assert ns.n <= NODE_STEPS
                if ns.n < NODE_STEPS:
                    dve.sem_inc(nv, NODE_STEPS - ns.n)

            ns = Steps(nv, L * NODE_STEPS)
            ns.done(v.tensor_tensor(total[:], total[:], x_cur[:], ALU.add))
            ns.wait(dve)

            def layer_norm(to3, z3, centered3, tmp3, r):
                ns.done(v.tensor_reduce(nodeA[:], z3, AX_X, ALU.add))
                ns.wait(dve)
                ns.done(v.tensor_scalar(nodeA[:], nodeA[:], 1.0 / C, None, ALU.mult))
                ns.wait(dve)
                ns.done(v.tensor_tensor(centered3, z3, per_node(nodeA[:]), ALU.subtract))
                ns.wait(dve)
                ns.done(v.tensor_tensor(tmp3, centered3, centered3, ALU.mult))
                ns.wait(dve)
                ns.done(v.tensor_reduce(nodeA[:], tmp3, AX_X, ALU.add))
                ns.wait(dve)
                ns.done(v.tensor_scalar(nodeA[:], nodeA[:], 1.0 / C, EPS, ALU.mult, ALU.add))
                ns.wait(dve)
                dve.sem_inc(root_in, 1)
                dve.wait_ge(root_done, r)
                ns.done(v.reciprocal(nodeA[:], nodeB[:]))
                ns.wait(dve)
                ns.done(v.tensor_tensor(to3, centered3, per_node(nodeA[:]), ALU.mult))
                ns.wait(dve)

            layer_norm(x3, t3, a3, p3, L + 1)
            ns.done(v.tensor_scalar(nodeA[:], rs[:, :, NPL], 1.0, None, ALU.max))
            ns.wait(dve)
            dve.sem_inc(root_in, 1)
            dve.wait_ge(root_done, L + 2)
            ns.done(v.reciprocal(nodeA[:], nodeB[:]))
            ns.wait(dve)
            ns.done(v.scalar_tensor_tensor(dinv[:], rs[:, :, NPL], 1.0, nodeA[:], ALU.min, ALU.mult))
            ns.wait(dve)
            dve.wait_ge(xd_out, L * 32)
            make_xd()
            ns.done(v.memset(acc[:], 0.0))
            ns.done(v.memset(mask_all[:], 1.0))
            ns.wait(dve)
            segment_adds(L, False)
            dve.wait_ge(seg_added, (L + 1) * (n_it + 1) * BP + 1)
            ns.done(v.tensor_tensor(p3, a3, per_node(dinv[:]), ALU.mult))
            ns.wait(dve)
            dve.wait_ge(xd_out, (L + 1) * 32)
            with dve.Fori(0, NCH // 2) as j:
                c0 = dve.snap(j * 2)
                H = dve.snap((c0 + L * NCH) * 2)
                for s in range(2):
                    dve.wait_ge(xT_ps, H + 2 * s)
                    v.tensor_copy(xs[:, s, :], p_f32[:, bass.ds((c0 + s) * (CB * C), CB * C)]).then_inc(xs_ready, 1)
                for s in range(2):
                    for h, (first, n) in enumerate(HALVES):
                        dve.wait_ge(f_ps, H + 2 * s + h + 3)
                        v.tensor_tensor(stage[:, bass.ds((c0 + s) * (CB * C) + first * C, n * C)].rearrange(view, c=C),
                                        banks[2 + h][:, 0:n * C].rearrange(view, c=C),
                                        b1[:].unsqueeze(1).to_broadcast([P, n, C]), ALU.add).then_inc(pq_read, 1)
            dve.wait_ge(pq_read, (L + 1) * NCH * 2 + 2)
            ns.done(v.scalar_tensor_tensor(total[:], stage[:], 0.0, x_cur[:], ALU.max, ALU.add))
            ns.wait(dve)
            layer_norm(a3, t3, s3, p3, L + 3)
            dve.sem_inc(out_ready, 1)


_INS = ['x', 'src', 'dst', 'L0_gnn_nb_W', 'L0_gnn_nb_b', 'L0_gnn_self_W', 'L0_gnn_self_b', 'L0_gnn_att1_W',
        'L0_gnn_att1_b', 'L0_gnn_att2_W', 'L0_gnn_att2_b', 'L1_gnn_weight', 'L1_gnn_bias']


def kernel(**inputs):
    import numpy as np
    import concourse.bacc as bacc
    from concourse.bass_utils import run_bass_kernel_spmd

    nc = bacc.Bacc("TRN2", target_bir_lowering=False, num_devices=1)
    arrays, args = {}, []
    for name in _INS:
        a = np.ascontiguousarray(inputs[name])
        arrays[f"in_{name}"] = a
        args.append(nc.dram_tensor(f"in_{name}", a.shape, mybir.dt.from_np(a.dtype), kind="ExternalInput").ap())
    out = nc.dram_tensor("out_0", inputs['x'].shape, F32, kind="ExternalOutput").ap()
    gnn_kernel(nc, *args, out)
    r = run_bass_kernel_spmd(nc, [arrays], core_ids=[0])
    return r.results[0]["out_0"]
```
